# Optimizing a Trainium2 kernel written in Bass

```python
import numpy as np
import jax
import jax.numpy as jnp

def _softmax(x, axis=-1):
    return jax.nn.softmax(x, axis=axis)

def _gelu(x):
    return jax.nn.gelu(x, approximate=True)

def _silu(x):
    return jax.nn.silu(x)

def _sigmoid(x):
    return jax.nn.sigmoid(x)

def _layernorm(x, axis=-1, eps=1e-05):
    m = jnp.mean(x, axis=axis, keepdims=True)
    v = jnp.var(x, axis=axis, keepdims=True)
    return (x - m) / jnp.sqrt(v + eps)

def _scatter_add(tgt, idx, src, axis=0):
    return tgt.at[idx].add(src)

def _segment_sum(src, seg, n):
    return jax.ops.segment_sum(src, seg, n)
kernel_name = 'mk_macaron_d1_jaxref_r8_f149ac'

def setup_inputs(seed: int=0):
    np.random.seed(seed)
    _w = jnp.asarray

    def _L0_attn_setup():
        import jax, jax.numpy as jnp
        import numpy as np
        H = 512
        D = H // 4
        key = jax.random.key(seed)
        k1, k2, k3, k4, k5 = jax.random.split(key, 5)
        x = jax.random.normal(k1, (4, 512, H), dtype=jnp.float32)
        s_in = 1.0 / np.sqrt(H)
        Wqkv = jax.random.normal(k2, (H, 3 * D), dtype=jnp.float32) * s_in
        bqkv = jax.random.normal(k3, (3 * D,), dtype=jnp.float32) * 0.01
        Wo = jax.random.normal(k4, (D, H), dtype=jnp.float32) * (1.0 / np.sqrt(D))
        bo = jax.random.normal(k5, (H,), dtype=jnp.float32) * 0.01
        return {'x': x, 'Wqkv': Wqkv, 'bqkv': bqkv, 'Wo': Wo, 'bo': bo}
    _L0_attn_in = _L0_attn_setup()

    def _L0_ffn_setup():
        import jax, jax.numpy as jnp
        import numpy as np
        TOP_K = 2
        key = jax.random.key(seed)
        k0, k1, k2 = jax.random.split(key, 3)
        B, S, D, H, E = (4, 256, 512, 512, 8)
        sc = 1.0 / np.sqrt(D).astype(np.float32)
        x = jax.random.normal(k0, (B, S, D), dtype=jnp.float32)
        W_gate = jax.random.normal(k1, (D, E), dtype=jnp.float32) * sc
        b_gate = jnp.zeros((E,), dtype=jnp.float32)
        W_e = jax.random.normal(k2, (E, D, H), dtype=jnp.float32) * sc
        b_e = jnp.zeros((E, H), dtype=jnp.float32)
        return {'x': x, 'W_gate': W_gate, 'b_gate': b_gate, 'W_e': W_e, 'b_e': b_e}
    _L0_ffn_in = _L0_ffn_setup()
    _d = {'L0_attn_x': _L0_attn_in['x'], 'L0_attn_Wqkv': _L0_attn_in['Wqkv'], 'L0_attn_bqkv': _L0_attn_in['bqkv'], 'L0_attn_Wo': _L0_attn_in['Wo'], 'L0_attn_bo': _L0_attn_in['bo'], 'L0_ffn_W_gate': _L0_ffn_in['W_gate'], 'L0_ffn_b_gate': _L0_ffn_in['b_gate'], 'L0_ffn_W_e': _L0_ffn_in['W_e'], 'L0_ffn_b_e': _L0_ffn_in['b_e']}
    _x0 = _d['L0_attn_x']
    _d['L0_attn_x'] = jax.random.normal(jax.random.fold_in(jax.random.key(seed), 1), (4, 256, 512), dtype=_x0.dtype)
    del _x0
    return _d

def reference(L0_attn_x, L0_attn_Wqkv, L0_attn_bqkv, L0_attn_Wo, L0_attn_bo, L0_ffn_W_gate, L0_ffn_b_gate, L0_ffn_W_e, L0_ffn_b_e):

    def _L0_attn_ref(x, Wqkv, bqkv, Wo, bo):
        import jax, jax.numpy as jnp
        import numpy as np
        H = 512
        D = H // 4
        B, S, C = x.shape
        d = C // 4
        qkv = jnp.einsum('bsc,cf->bsf', x, Wqkv) + bqkv
        qkv = qkv.reshape(B, S, 3, d)
        q, k, v = (qkv[:, :, 0], qkv[:, :, 1], qkv[:, :, 2])
        scale = 1.0 / jnp.sqrt(jnp.float32(d)).astype(x.dtype)
        attn = jnp.einsum('bqd,bkd->bqk', q, k) * scale
        attn = jax.nn.softmax(attn, axis=-1)
        out = jnp.einsum('bqk,bkd->bqd', attn, v)
        return jnp.einsum('bqd,dc->bqc', out, Wo) + bo

    def _L0_ffn_ref(x, W_gate, b_gate, W_e, b_e):
        import jax, jax.numpy as jnp
        import numpy as np
        TOP_K = 2
        logits = x @ W_gate + b_gate
        _, top_idx = jax.lax.top_k(logits, TOP_K)
        y_all = jax.nn.relu(jnp.einsum('bsd,edh->bseh', x, W_e) + b_e)
        y = jnp.take_along_axis(y_all, top_idx[..., None], axis=2)
        return y.mean(axis=2)
    x = L0_attn_x
    x = x + 0.5 * _L0_ffn_ref(_layernorm(x, axis=-1), L0_ffn_W_gate, L0_ffn_b_gate, L0_ffn_W_e, L0_ffn_b_e)
    x = x + _L0_attn_ref(_layernorm(x, axis=-1), L0_attn_Wqkv, L0_attn_bqkv, L0_attn_Wo, L0_attn_bo)
    x = x + 0.5 * _L0_ffn_ref(_layernorm(x, axis=-1), L0_ffn_W_gate, L0_ffn_b_gate, L0_ffn_W_e, L0_ffn_b_e)
    return x

_drawn_inputs = setup_inputs


def setup_inputs(seed=0):
    import zlib

    import numpy as np

    out = dict(_drawn_inputs(seed))
    spreads = {'L0_ffn_b_gate': (0.0, 0.1), 'L0_ffn_b_e': (0.0, 0.1)}
    factors = {'L0_attn_bqkv': 2.964, 'L0_attn_bo': 4.171}
    for name, (base, spread) in spreads.items():
        noise = np.random.default_rng([zlib.crc32(name.encode()), seed]).standard_normal(out[name].shape)
        drawn = base * np.exp(spread * noise) if base else spread * noise
        out[name] = jnp.asarray(drawn.astype(out[name].dtype))
    for name, factor in factors.items():
        out[name] = (out[name] * factor).astype(out[name].dtype)
    return out
```

```python
from contextlib import ExitStack

import concourse.bass as bass
from concourse import mybir

P = 128
ALU = mybir.AluOpType
ACT = mybir.ActivationFunctionType
F32 = mybir.dt.float32
BF16 = mybir.dt.bfloat16
I32 = mybir.dt.int32
U32 = mybir.dt.uint32
AX_X = mybir.AxisListType.X
EPS = 1e-5
TOP_K = 2


def macaron_kernel(nc, x_in, w_qkv, b_qkv, w_o, b_o, w_gate, b_gate, w_e, b_e, out):
    B, S, H = x_in.shape
    E, _, HO = w_e.shape
    D = w_o.shape[0]
    T = B * S
    NT = T // P
    NC = H // P
    TB = S // P
    NS = T * TOP_K // P + E - 1
    SCALE = float(D) ** -0.5
    HALF_MEAN = 0.5 / TOP_K
    assert S == 2 * P and D == P and HO == H and H <= 512 and NS % 2 == 1 and T // P <= 8

    x_rows = x_in.rearrange("b s h -> (b s) h")
    out_rows = out.rearrange("b s h -> (b s) h")

    with ExitStack() as ctx:
        def sb(name, shape, dt=F32):
            return ctx.enter_context(nc.sbuf_tensor(name, shape, dt))

        def psum(name, shape):
            return ctx.enter_context(nc.psum_tensor(name, shape, F32))

        def sem(name):
            return ctx.enter_context(nc.semaphore(name))

        xn_dram = [nc.dram_tensor(f"xn_dram{f}", [T, H], F32, kind="Internal") for f in range(2)]
        y_dram = [nc.dram_tensor(f"y_dram{f}", [NS * P, H], F32, kind="Internal") for f in range(2)]

        XN, XG, CG, YB = 4, 4, 8, 3
        x = sb("x", [P, NT, H])
        wexp = sb("wexp", [P, E * NC * H])
        be_bc = sb("be_bc", [P, E * H])
        wqkv = sb("wqkv", [P, NC, 3 * D])
        wo = sb("wo", [P, H])
        wg = sb("wg", [P, NC, E])
        bg_bc = sb("bg_bc", [P, E])
        bo_bc = sb("bo_bc", [P, H])
        bv_bc = sb("bv_bc", [P, D])
        bqk = sb("bqk", [P, 2])
        xn = sb("xn", [P, XN, H])
        xt_gate = sb("xt_gate", [P, 2, H])
        xt_att = sb("xt_att", [P, NC, S])
        xg = sb("xg", [P, XG, H])
        xt_exp = sb("xt_exp", [P, 2, H])
        ypre = sb("ypre", [P, 2, H])
        yrow = sb("yrow", [P, YB, H])
        cg = sb("cg", [P, CG, H])
        stats = sb("stats", [P, XN, 6])
        mv = sb("mv", [P, XN, 2])
        var_eps = sb("var_eps", [P, XN])
        rstd = sb("rstd", [P, XN])
        neg_half = sb("neg_half", [P, TB])
        logit = sb("logit", [P, E])
        top = sb("top", [P, 8])
        topi = sb("topi", [P, 8], U32)
        topf = sb("topf", [P, TOP_K])
        onehot = sb("onehot", [P, NT, TOP_K, E], BF16)
        ident = sb("ident", [P, P])
        before = sb("before", [P, P], BF16)
        ones = sb("ones", [P, P], BF16)
        iota_e = sb("iota_e", [P, E])
        iota_r = sb("iota_r", [P, P], BF16)
        iota_t = sb("iota_t", [P, NS])
        thresh = sb("thresh", [P, E, NT])
        part_id = sb("part_id", [P, 1])
        tile_id = sb("tile_id", [P, NT * TOP_K])
        zeros_e = sb("zeros_e", [P, E])
        above = sb("above", [P, E, NT])
        ntile = sb("ntile", [P, E])
        incl = sb("incl", [P, E])
        excl = sb("excl", [P, E])
        slot_e = sb("slot_e", [P, NT, E])
        picked = sb("picked", [P, NT, TOP_K, E])
        slot = sb("slot", [P, NT * TOP_K])
        slot_u = sb("slot_u", [P, NT * TOP_K], U32)
        slot_bits = sb("slot_bits", [P, NT * TOP_K], U32)
        slot_r = sb("slot_r", [P, NT * TOP_K])
        slot_t = sb("slot_t", [P, NT * TOP_K])
        in_tile = sb("in_tile", [P, NT * TOP_K, NS])
        mark = sb("mark", [P, NT * TOP_K, 2, NS], BF16)
        row_hot = sb("row_hot", [P, NT * TOP_K, P], BF16)
        tok_lo = sb("tok_lo", [P, NS])
        tok = sb("tok", [P, NS], U32)
        passed = sb("passed", [1, NS, E])
        eid_f = sb("eid_f", [1, NS])
        eid_c = sb("eid_c", [1, NS])
        eid = sb("eid", [1, NS], I32)
        qk = sb("qk", [P, 2, S])
        v_ring = [sb(f"v{i}", [P, TB, D]) for i in range(2)]
        nmax = sb("nmax", [P, TB])
        smax = sb("smax", [P, TB])
        prob = sb("prob", [P, TB, S])
        psumrow = sb("psumrow", [P, TB])
        pinv = sb("pinv", [P, TB])
        pt = sb("pt", [P, TB, S])
        ot = sb("ot", [P, S])

        tp_ps = [psum(f"tp_ps{i}", [P, 512]) for i in range(2)]
        y0_ps = psum("y0_ps", [P, 512])
        qk_ps = psum("qk_ps", [P, 512])
        vo_ps = psum("vo_ps", [P, 512])
        sp_ps = psum("sp_ps", [P, 512])
        g_ps = psum("g_ps", [P, 512])
        rk_ps = psum("rk_ps", [P, 512])
        y_ps = [y0_ps, qk_ps]
        rank = rk_ps[:, 0:(NT + 1) * E].rearrange("p (t e) -> p t e", e=E)
        list_ps = g_ps[:, 0:2 * NS]

        SMALL = 6
        x_in_sem = [sem(f"x_loaded{b}") for b in range(B)]
        small_in = sem("small_loaded")
        be_in = sem("be_loaded")
        w_in = [sem(f"wexp_loaded{e}") for e in range(E)]
        att_w_in = sem("att_weights_loaded")
        const_made = sem("const_made")
        const_step = sem("const_step")
        dve_step = sem("dve_step")
        var_made = sem("var_made")
        rstd_made = sem("rstd_made")
        xn_made = sem("xn_made")
        xn_stored = [sem(f"xn_stored{s}") for s in range(XN)]
        tp_full = sem("tp_full")
        tp_copied = sem("tp_copied")
        gate_done = sem("gate_done")
        logit_read = sem("logit_read")
        onehot_made = sem("onehot_made")
        rank_done = sem("rank_done")
        slots_made = sem("slots_made")
        slots_u_made = sem("slots_u_made")
        mark_made = sem("mark_made")
        row_hot_made = sem("row_hot_made")
        list_done = sem("list_done")
        tok_made = sem("tok_made")
        eid_made = sem("eid_made")
        gathered = [sem(f"gathered{s}") for s in range(XG)]
        exp_done = sem("exp_done")
        ypre_made = sem("ypre_made")
        yrow_made = sem("yrow_made")
        y_stored = [sem(f"y_stored{s}") for s in range(YB)]
        back = [sem(f"back{s}") for s in range(CG)]
        x_ffn = sem("x_ffn")
        bo_added = sem("bo_added")
        qk_done = sem("qk_done")
        qk_copied = sem("qk_copied")
        v_done = sem("v_done")
        v_made = sem("v_made")
        score_done = sem("score_done")
        nmax_made = sem("nmax_made")
        prob_made = sem("prob_made")
        pt_done = sem("pt_done")
        pt_copied = sem("pt_copied")
        ot_done = sem("ot_done")
        ot_copied = sem("ot_copied")
        wo_done = sem("wo_done")
        x_att = sem("x_att")
        out_stored = sem("out_stored")

        uses = [("g0", i) for i in range(NT)] + [("exp0", t) for t in range(NS)]
        norms = [("g0", i) for i in range(NT)]
        uses += [("att", i) for i in range(TB)]
        norms += [("att", i) for i in range(TB)]
        for b in range(B):
            if b + 1 < B:
                uses += [("att", i) for i in range(TB * (b + 1), TB * (b + 2))]
                norms += [("att", i) for i in range(TB * (b + 1), TB * (b + 2))]
            if b >= 1:
                uses += [("g1", i) for i in range(TB * (b - 1), TB * b)]
            norms += [("g1", i) for i in range(TB * b, TB * (b + 1))]
        uses += [("g1", i) for i in range(TB * (B - 1), NT)] + [("exp1", t) for t in range(NS)]
        use_no = {u: n for n, u in enumerate(uses)}
        norm_no = {u: n for n, u in enumerate(norms)}
        stores_before, in_slot = [], [0] * XN
        for n, (kind, _) in enumerate(norms):
            stores_before.append(in_slot[n % XN])
            if kind != "att":
                in_slot[n % XN] += 1

        block = ctx.enter_context(nc.Block())

        @block.sync
        def _(sp):
            for b in range(B):
                sp.dma_start(x[:, TB * b:TB * (b + 1), :],
                             x_rows[b * S:(b + 1) * S, :].rearrange("(t p) h -> p t h", p=P)
                             ).then_inc(x_in_sem[b], 16)

            def load_expert(e):
                sp.dma_start(wexp[:, e * NC * H:(e + 1) * NC * H].rearrange("p (c h) -> p c h", c=NC),
                             w_e[e].rearrange("(c p) h -> p c h", p=P)).then_inc(w_in[e], 16)

            def store_xn(f, i):
                n = norm_no[(f"g{f}", i)]
                sp.wait_ge(xn_made, n + 1)
                sp.dma_start(xn_dram[f][i * P:(i + 1) * P, :], xn[:, n % XN, :]
                             ).then_inc(xn_stored[n % XN], 16)

            def store_y(f, t, slot_no, made):
                sp.wait_ge(yrow_made, made)
                sp.dma_start(y_dram[f][bass.ds(t * P, P), :], yrow[:, slot_no, :]
                             ).then_inc(y_stored[slot_no], 16)

            load_expert(0)
            load_expert(1)
            for i in range(NT):
                store_xn(0, i)
                if i + 2 < E:
                    load_expert(i + 2)
            sp.dma_start(wqkv[:], w_qkv.rearrange("(c p) n -> p c n", p=P)).then_inc(att_w_in, 16)
            sp.dma_start(wo[:], w_o).then_inc(att_w_in, 16)
            for f in range(2):
                if f == 1:
                    for i in range(NT):
                        store_xn(1, i)
                whole = NS // YB * YB
                with sp.Fori(0, whole, YB) as t0:
                    for j in range(YB):
                        store_y(f, t0 + j, j, t0 + (f * NS + j + 1))
                for t in range(whole, NS):
                    store_y(f, t, t % YB, f * NS + t + 1)
            for i in range(NT):
                sp.wait_ge(x_ffn, NT + i + 1)
                sp.dma_start(out_rows[i * P:(i + 1) * P, :], x[:, i, :]).then_inc(out_stored, 16)
            sp.wait_ge(out_stored, 16 * NT)

        @block.gpsimd
        def _(pool):
            steps = [0]

            def link(ins):
                steps[0] += 1
                ins.then_inc(const_step, 1)
                pool.wait_ge(const_step, steps[0])

            link(pool.memset(ident[:], 0.0))
            pool.affine_select(out=ident[:], in_=ident[:], compare_op=ALU.not_equal, fill=1.0, base=0,
                               pattern=[[-1, P]], channel_multiplier=1).then_inc(const_made, 1)
            pool.iota(iota_e[:], pattern=[[1, E]], base=0, channel_multiplier=0,
                      allow_small_or_imprecise_dtypes=True).then_inc(const_made, 1)
            link(pool.memset(ones[:], 1.0))
            pool.affine_select(out=before[:], in_=ones[:], compare_op=ALU.is_gt, fill=0.0, base=0,
                               pattern=[[1, P]], channel_multiplier=-1).then_inc(const_made, 1)
            pool.iota(iota_r[:], pattern=[[1, P]], base=0, channel_multiplier=0,
                      allow_small_or_imprecise_dtypes=True).then_inc(const_made, 1)
            pool.iota(iota_t[:], pattern=[[1, NS]], base=0, channel_multiplier=0,
                      allow_small_or_imprecise_dtypes=True).then_inc(const_made, 1)
            pool.iota(thresh[:], pattern=[[0, E], [P, NT]], base=0, channel_multiplier=0,
                      allow_small_or_imprecise_dtypes=True).then_inc(const_made, 1)
            pool.iota(part_id[:], pattern=[[0, 1]], base=0, channel_multiplier=1,
                      allow_small_or_imprecise_dtypes=True).then_inc(const_made, 1)
            pool.iota(tile_id[:].rearrange("p (t k) -> p t k", k=TOP_K), pattern=[[1, NT], [0, TOP_K]],
                      base=0, channel_multiplier=0,
                      allow_small_or_imprecise_dtypes=True).then_inc(const_made, 1)
            pool.memset(zeros_e[:], 0.0).then_inc(const_made, 1)
            link(pool.memset(neg_half[:], -0.5))

            def deviations(kind, b):
                n = norm_no[(kind, TB * b)]
                s = n % XN
                pool.wait_ge(var_made, n // TB + 1)
                if n >= XN:
                    pool.wait_ge(xn_made, n - XN + TB)
                pool.tensor_tensor(rstd[:, s:s + TB], var_eps[:, s:s + TB], neg_half[:], ALU.pow
                                   ).then_inc(rstd_made, 1)

            def gather_tokens(f):
                pool.wait_ge(tok_made, f + 1)
                for s in range(XN):
                    pool.wait_ge(xn_stored[s], 16 * stored_by(f)[s])
                for t in range(NS):
                    n = f * NS + t
                    if t >= XG:
                        pool.wait_ge(tp_full, use_no[(f"exp{f}", t - XG)] + 1)
                    elif f:
                        pool.wait_ge(tp_full, use_no[("exp0", NS - 1)] + 1)
                    pool.indirect_dma_start(
                        out=xg[:, n % XG, :], out_offset=None, in_=xn_dram[f][:, :],
                        in_offset=bass.IndirectOffsetOnAxis(ap=tok[:, t:t + 1], axis=0)
                    ).then_inc(gathered[n % XG], 16)

            def stored_by(f):
                count = [0] * XN
                for n, (kind, _) in enumerate(norms):
                    if kind == "g0" or (kind == "g1" and f):
                        count[n % XN] += 1
                return count

            def gather_back(f, i):
                for k in range(TOP_K):
                    m = (f * NT + i) * TOP_K + k
                    if m >= CG:
                        pool.wait_ge(x_ffn, (m - CG) // TOP_K + 1)
                    j = i * TOP_K + k
                    pool.indirect_dma_start(
                        out=cg[:, m % CG, :], out_offset=None, in_=y_dram[f][:, :],
                        in_offset=bass.IndirectOffsetOnAxis(ap=slot_u[:, j:j + 1], axis=0)
                    ).then_inc(back[m % CG], 16)

            def wait_y(f):
                whole = (NS + YB - 1) // YB * YB
                for s in range(YB):
                    n = sum(1 for t in range(NS) if t % YB == s)
                    pool.wait_ge(y_stored[s], 16 * (f + 1) * n)

            def add_bo(b):
                for i in range(TB * b, TB * (b + 1)):
                    pool.wait_ge(xn_made, norm_no[("att", i)] + 1)
                    if i == 0:
                        pool.wait_ge(small_in, 16 * SMALL)
                    pool.tensor_tensor(x[:, i, :], x[:, i, :], bo_bc[:], ALU.add).then_inc(bo_added, 1)

            for b in range(B):
                deviations("g0", b)
            gather_tokens(0)
            wait_y(0)
            pool.wait_ge(slots_u_made, 1)
            for i in range(2 * TB):
                gather_back(0, i)
            deviations("att", 0)
            add_bo(0)
            for b in range(B):
                if b + 1 < B:
                    deviations("att", b + 1)
                    add_bo(b + 1)
                if b + 2 < B:
                    for i in range(TB * (b + 2), TB * (b + 3)):
                        gather_back(0, i)
                deviations("g1", b)
            gather_tokens(1)
            wait_y(1)
            pool.wait_ge(slots_u_made, 2)
            for i in range(NT):
                gather_back(1, i)

        @block.scalar
        def _(act):
            act.dma_start(wg[:], w_gate.rearrange("(c p) e -> p c e", p=P)).then_inc(small_in, 16)
            act.dma_start(bg_bc[:], b_gate.partition_broadcast(P)).then_inc(small_in, 16)
            act.dma_start(bqk[:], b_qkv[0:2 * D].rearrange("(j d) -> d j", j=2),
                          allow_slow_non_contiguous=True).then_inc(small_in, 16)
            act.dma_start(bv_bc[:], b_qkv[2 * D:3 * D].partition_broadcast(P)).then_inc(small_in, 16)
            act.dma_start(bo_bc[:], b_o.partition_broadcast(P)).then_inc(small_in, 16)
            act.dma_start(be_bc[:], b_e.rearrange("e h -> (e h)").partition_broadcast(P)
                          ).then_inc(small_in, 16)

            def copy_gate(f, i):
                n = use_no[(f"g{f}", i)]
                if f * NT + i >= 2:
                    act.wait_ge(gate_done, f * NT + i - 1)
                act.wait_ge(tp_full, n + 1)
                act.activation(xt_gate[:, i % 2, :], tp_ps[n % 2][:], ACT.Copy).then_inc(tp_copied, 1)

            def copy_att(i):
                n = use_no[("att", i)]
                b = i // TB
                if b:
                    act.wait_ge(v_done, b)
                act.wait_ge(tp_full, n + 1)
                act.activation(xt_att[:, :, (i % TB) * P:(i % TB + 1) * P],
                               tp_ps[n % 2][:].rearrange("p (c t) -> p c t", c=NC),
                               ACT.Copy).then_inc(tp_copied, 1)

            def copy_exp(f, bank, slot_no, full, free):
                act.wait_ge(tp_full, full)
                if free is not None:
                    act.wait_ge(exp_done, free)
                act.activation(xt_exp[:, slot_no, :], tp_ps[bank][:], ACT.Copy).then_inc(tp_copied, 1)

            def relu_y(slot2, slot_no, made, stored):
                act.wait_ge(ypre_made, made)
                if stored is not None:
                    act.wait_ge(y_stored[slot_no], stored)
                act.activation(yrow[:, slot_no, :], ypre[:, slot2, :], ACT.Relu,
                               scale=HALF_MEAN).then_inc(yrow_made, 1)

            def experts(f):
                n0 = use_no[(f"exp{f}", 0)]
                per = [sum(1 for t in range(NS) if t % YB == s) for s in range(YB)]

                def tile(t):
                    if t + 1 < NS:
                        free = f * NS + t if f or t >= 1 else None
                        copy_exp(f, (n0 + t + 1) % 2, (t + 1) % 2, n0 + t + 2, free)
                    stored = 16 * (f * per[t % YB] + t // YB)
                    relu_y(t % 2, t % YB, f * NS + t + 1, stored if stored else None)

                copy_exp(f, n0 % 2, 0, n0 + 1, f * NS - 1 if f else None)
                head = 2 * YB
                step = 2 * YB
                for t in range(head):
                    tile(t)
                loops = (NS - 1 - head) // step
                with act.Fori(0, loops) as r:
                    for j in range(step):
                        t = head + j
                        copy_exp(f, (n0 + t + 1) % 2, (t + 1) % 2, r * step + (n0 + t + 2),
                                 r * step + (f * NS + t))
                        relu_y(t % 2, t % YB, r * step + (f * NS + t + 1),
                               r * (16 * step // YB) + 16 * (f * per[t % YB] + t // YB))
                for t in range(head + loops * step, NS):
                    tile(t)

            def copy_qk(b):
                act.wait_ge(qk_done, b + 1)
                if b:
                    act.wait_ge(score_done, b)
                for j in range(2):
                    act.activation(qk[:, j, :], qk_ps[:, j * S:(j + 1) * S], ACT.Identity,
                                   bias=bqk[:, j:j + 1]).then_inc(qk_copied, 1)

            def softmax(b):
                act.wait_ge(nmax_made, b + 1)
                if b:
                    act.wait_ge(pt_done, b)
                    act.wait_ge(x_att, TB * b)
                for q in range(TB):
                    act.activation(prob[:, q, :], sp_ps[:, q * S:(q + 1) * S], ACT.Exp,
                                   bias=nmax[:, q:q + 1], scale=SCALE,
                                   accum_out=psumrow[:, q:q + 1]).then_inc(prob_made, 1)

            act.wait_ge(const_made, 9)
            for i in range(NT):
                copy_gate(0, i)
            experts(0)
            act.wait_ge(small_in, 16 * SMALL)
            for i in range(TB):
                copy_att(i)
            copy_qk(0)
            for b in range(B):
                softmax(b)
                if b + 1 < B:
                    for i in range(TB * (b + 1), TB * (b + 2)):
                        copy_att(i)
                if b >= 1:
                    for i in range(TB * (b - 1), TB * b):
                        copy_gate(1, i)
                if b + 1 < B:
                    copy_qk(b + 1)
                act.wait_ge(pt_done, b + 1)
                if b:
                    act.wait_ge(ot_done, b)
                act.activation(pt[:].rearrange("p t s -> p (t s)"), sp_ps[:], ACT.Copy
                               ).then_inc(pt_copied, 1)
                act.wait_ge(ot_done, b + 1)
                if b:
                    act.wait_ge(wo_done, TB * b)
                act.activation(ot[:], vo_ps[:, 0:S], ACT.Copy).then_inc(ot_copied, 1)
            for i in range(TB * (B - 1), NT):
                copy_gate(1, i)
            experts(1)

        @block.tensor
        def _(pe):
            def transpose_rows(n, rows):
                if n >= 2:
                    pe.wait_ge(tp_copied, n - 1)
                for c in range(NC):
                    last = pe.transpose(tp_ps[n % 2][:, c * P:(c + 1) * P], rows[:, c * P:(c + 1) * P],
                                        ident[:])
                last.then_inc(tp_full, 1)

            def transpose_xn(kind, i):
                m = norm_no[(kind, i)]
                pe.wait_ge(xn_made, m + 1)
                transpose_rows(use_no[(kind, i)], xn[:, m % XN, :])

            def gate(f, i):
                pe.wait_ge(tp_copied, use_no[(f"g{f}", i)] + 1)
                if f * NT + i:
                    pe.wait_ge(logit_read, f * NT + i)
                for c in range(NC):
                    last = pe.matmul(g_ps[:, 0:E], xt_gate[:, i % 2, c * P:(c + 1) * P], wg[:, c, :],
                                     start=(c == 0), stop=(c == NC - 1))
                last.then_inc(gate_done, 1)

            def count(f, i):
                pe.wait_ge(onehot_made, f * NT + i + 1)
                if f and i == 0:
                    pe.wait_ge(slots_made, 1)
                for k in range(TOP_K):
                    pe.matmul(rank[:, i, :], before[:], onehot[:, i, k, :],
                              start=(i == 0 and k == 0), stop=False, skip_group_check=True)
                    rest = onehot[:, i, k, :].unsqueeze(1).broadcast_to([P, NT - i, E])
                    last = pe.matmul(rank[:, i + 1:NT + 1, :], ones[:], rest,
                                     start=False, stop=(i == NT - 1 and k == TOP_K - 1),
                                     skip_group_check=True)
                if i == NT - 1:
                    last.then_inc(rank_done, 1)

            def token_list(f):
                pe.wait_ge(mark_made, f + 1)
                for j in range(NT * TOP_K):
                    pe.wait_ge(row_hot_made, f * NT * TOP_K + j + 1)
                    last = pe.matmul(list_ps, row_hot[:, j, :],
                                     mark[:, j, :, :].rearrange("p a t -> p (a t)"),
                                     start=(j == 0), stop=(j == NT * TOP_K - 1))
                last.then_inc(list_done, 1)

            def experts(f):
                n0 = use_no[(f"exp{f}", 0)]

                def transposes(n, slot_no, full, copied, landed):
                    pe.wait_ge(gathered[slot_no], landed)
                    pe.wait_ge(tp_copied, copied)
                    for c in range(NC):
                        last = pe.transpose(tp_ps[n % 2][:, c * P:(c + 1) * P],
                                            xg[:, slot_no, c * P:(c + 1) * P], ident[:])
                    last.then_inc(tp_full, 1)

                def product(t, t_mod, copied, read):
                    e = pe.value_load(eid[0:1, bass.ds(t, 1)], min_val=0, max_val=E - 1)
                    pe.wait_ge(tp_copied, copied)
                    if read is not None:
                        pe.wait_ge(ypre_made, read)
                    for c in range(NC):
                        last = pe.matmul(y_ps[t_mod % 2][:], xt_exp[:, t_mod % 2, c * P:(c + 1) * P],
                                         wexp[:, bass.ds(e * (NC * H) + c * H, H)],
                                         start=(c == 0), stop=(c == NC - 1))
                    last.then_inc(exp_done, 1)

                def landed(t):
                    n = f * NS + t
                    return 16 * (n // XG + 1)

                transposes(n0, f * NS % XG, n0 + 1, n0 - 1, landed(0))
                pe.wait_ge(eid_made, f + 1)
                if f == 0:
                    for e in range(E):
                        pe.wait_ge(w_in[e], 16)
                head = 4
                step = 4

                def tile(t):
                    if t + 1 < NS:
                        transposes(n0 + t + 1, (f * NS + t + 1) % XG, n0 + t + 2, n0 + t, landed(t + 1))
                    read = f * NS + t - 1
                    product(t, t, n0 + t + 1, read if read > 0 else None)

                for t in range(head):
                    tile(t)
                loops = (NS - 1 - head) // step
                with pe.Fori(0, loops) as r:
                    for j in range(step):
                        t = head + j
                        transposes(n0 + t + 1, (f * NS + t + 1) % XG, None, r * step + (n0 + t),
                                   r * (16 * step // XG) + landed(t + 1))
                        product(r * step + t, t, r * step + (n0 + t + 1), r * step + (f * NS + t - 1))
                for t in range(head + loops * step, NS):
                    tile(t)

            def project_qk(b):
                pe.wait_ge(tp_copied, use_no[("att", TB * (b + 1) - 1)] + 1)
                if b:
                    pe.wait_ge(qk_copied, 2 * b)
                else:
                    pe.wait_ge(ypre_made, NS)
                for j in range(2):
                    for c in range(NC):
                        last = pe.matmul(qk_ps[:, j * S:(j + 1) * S], wqkv[:, c, j * D:(j + 1) * D],
                                         xt_att[:, c, :], start=(c == 0), stop=(c == NC - 1))
                last.then_inc(qk_done, 1)

            def project_v(b):
                if b >= 2:
                    pe.wait_ge(ot_copied, b - 1)
                for i in range(TB):
                    for c in range(NC):
                        last = pe.matmul(vo_ps[:, i * D:(i + 1) * D], xt_att[:, c, i * P:(i + 1) * P],
                                         wqkv[:, c, 2 * D:3 * D], start=(c == 0), stop=(c == NC - 1))
                last.then_inc(v_done, 1)

            def scores(b):
                pe.wait_ge(qk_copied, 2 * (b + 1))
                if b:
                    pe.wait_ge(pt_copied, b)
                for q in range(TB):
                    last = pe.matmul(sp_ps[:, q * S:(q + 1) * S], qk[:, 0, q * P:(q + 1) * P],
                                     qk[:, 1, :], start=True, stop=True)
                last.then_inc(score_done, 1)

            def transpose_prob(b):
                pe.wait_ge(prob_made, TB * (b + 1))
                for k in range(TB):
                    for q in range(TB):
                        last = pe.transpose(sp_ps[:, k * S + q * P:k * S + (q + 1) * P],
                                            prob[:, q, k * P:(k + 1) * P], ident[:])
                last.then_inc(pt_done, 1)

            def mix_v(b):
                pe.wait_ge(pt_copied, b + 1)
                pe.wait_ge(v_made, min(b + 2, B))
                for k in range(TB):
                    last = pe.matmul(vo_ps[:, 0:S], v_ring[b % 2][:, k, :], pt[:, k, :],
                                     start=(k == 0), stop=(k == TB - 1))
                last.then_inc(ot_done, 1)

            def project_out(b):
                pe.wait_ge(ot_copied, b + 1)
                for q in range(TB):
                    n = TB * b + q
                    if n:
                        pe.wait_ge(x_att, n)
                    pe.matmul(y0_ps[:], ot[:, q * P:(q + 1) * P], wo[:], start=True, stop=True
                              ).then_inc(wo_done, 1)

            def front(f, tiles):
                for i in tiles:
                    transpose_xn(f"g{f}", i)
                    if i > tiles[0]:
                        gate(f, i - 1)
                    if i > tiles[0] + 1:
                        count(f, i - 2)
                gate(f, tiles[-1])
                if len(tiles) > 1:
                    count(f, tiles[-1] - 1)
                count(f, tiles[-1])

            pe.wait_ge(const_made, 9)
            pe.wait_ge(small_in, 16 * SMALL)
            front(0, list(range(NT)))
            token_list(0)
            experts(0)
            pe.wait_ge(att_w_in, 32)
            for i in range(TB):
                transpose_xn("att", i)
            project_qk(0)
            project_v(0)
            for b in range(B):
                scores(b)
                if b + 1 < B:
                    for i in range(TB * (b + 1), TB * (b + 2)):
                        transpose_xn("att", i)
                if b >= 1:
                    front(1, list(range(TB * (b - 1), TB * b)))
                if b + 1 < B:
                    project_qk(b + 1)
                transpose_prob(b)
                if b + 1 < B:
                    project_v(b + 1)
                mix_v(b)
                project_out(b)
            front(1, list(range(TB * (B - 1), NT)))
            token_list(1)
            experts(1)

        @block.vector
        def _(dve):
            steps = [0]

            def link(ins):
                steps[0] += 1
                ins.then_inc(dve_step, 1)
                dve.wait_ge(dve_step, steps[0])

            def moments(kind, b):
                n = norm_no[(kind, TB * b)]
                s = n % XN
                for i in range(TB):
                    link(dve.bn_stats(stats[:, s + i, :], x[:, TB * b + i, :]))
                    link(dve.bn_aggr(mv[:, s + i, :], stats[:, s + i, :]))
                if n >= XN:
                    dve.wait_ge(rstd_made, (n - XN) // TB + 1)
                dve.tensor_scalar(var_eps[:, s:s + TB], mv[:, s:s + TB, 1], EPS, None,
                                  ALU.add).then_inc(var_made, 1)

            def normalise(kind, i):
                n = norm_no[(kind, i)]
                s = n % XN
                if n >= XN:
                    dve.wait_ge(tp_full, use_no[norms[n - XN]] + 1)
                    if stores_before[n]:
                        dve.wait_ge(xn_stored[s], 16 * stores_before[n])
                dve.wait_ge(rstd_made, n // TB + 1)
                dve.tensor_scalar(xn[:, s, :], x[:, i, :], mv[:, s, 0:1], rstd[:, s:s + 1],
                                  ALU.subtract, ALU.mult).then_inc(xn_made, 1)

            def choose(f, i):
                dve.wait_ge(gate_done, f * NT + i + 1)
                ins = dve.tensor_tensor(logit[:], g_ps[:, 0:E], bg_bc[:], ALU.add)
                ins.then_inc(logit_read, 1)
                dve.wait_ge(logit_read, f * NT + i + 1)
                link(dve.max(top[:], logit[:]))
                link(dve.max_index(topi[:], top[:], logit[:]))
                link(dve.tensor_copy(topf[:], topi[:, 0:TOP_K]))
                dve.tensor_tensor(onehot[:, i, :, :],
                                  iota_e[:].unsqueeze(1).broadcast_to([P, TOP_K, E]),
                                  topf[:].unsqueeze(2).broadcast_to([P, TOP_K, E]),
                                  ALU.is_equal).then_inc(onehot_made, 1)

            def route(f):
                J = NT * TOP_K
                dve.wait_ge(rank_done, f + 1)
                link(dve.tensor_tensor(above[:], rank[:, NT, :].unsqueeze(2).broadcast_to([P, E, NT]),
                                       thresh[:], ALU.is_gt))
                link(dve.tensor_reduce(ntile[:], above[:], AX_X, ALU.add))
                link(dve.tensor_tensor_scan(incl[:], ntile[:], zeros_e[:], 0.0, ALU.add, ALU.add))
                link(dve.tensor_tensor(excl[:], incl[:], ntile[:], ALU.subtract))
                ins = dve.scalar_tensor_tensor(out=slot_e[:], in0=excl[:].unsqueeze(1).broadcast_to([P, NT, E]),
                                               scalar=float(P), in1=rank[:, 0:NT, :],
                                               op0=ALU.mult, op1=ALU.add)
                ins.then_inc(slots_made, 1)
                dve.wait_ge(slots_made, f + 1)
                link(dve.tensor_tensor(picked[:], onehot[:],
                                       slot_e[:].unsqueeze(2).broadcast_to([P, NT, TOP_K, E]), ALU.mult))
                link(dve.tensor_reduce(slot[:], picked[:].rearrange("p t k e -> p (t k) e"), AX_X, ALU.add))
                if f == 1:
                    dve.wait_ge(x_ffn, NT)
                ins = dve.tensor_copy(slot_u[:], slot[:])
                ins.then_inc(slots_u_made, 1)
                dve.wait_ge(slots_u_made, f + 1)
                link(dve.tensor_single_scalar(slot_bits[:], slot_u[:], P - 1, ALU.bitwise_and))
                link(dve.tensor_copy(slot_r[:], slot_bits[:]))
                for j in range(J):
                    dve.tensor_scalar(row_hot[:, j, :], iota_r[:], slot_r[:, j:j + 1], None,
                                      ALU.is_equal).then_inc(row_hot_made, 1)
                link(dve.tensor_tensor(slot_t[:], slot[:], slot_r[:], ALU.subtract))
                link(dve.tensor_scalar(slot_t[:], slot_t[:], 1.0 / P, None, ALU.mult))
                link(dve.tensor_tensor(in_tile[:], iota_t[:].unsqueeze(1).broadcast_to([P, J, NS]),
                                       slot_t[:].unsqueeze(2).broadcast_to([P, J, NS]), ALU.is_equal))
                link(dve.tensor_scalar(mark[:, :, 0, :], in_tile[:], part_id[:], None, ALU.mult))
                dve.tensor_tensor(mark[:, :, 1, :], in_tile[:],
                                  tile_id[:].unsqueeze(2).broadcast_to([P, J, NS]),
                                  ALU.mult).then_inc(mark_made, 1)
                link(dve.tensor_tensor(passed[:], iota_t[0:1, :].unsqueeze(2).broadcast_to([1, NS, E]),
                                       incl[0:1, :].unsqueeze(1).broadcast_to([1, NS, E]), ALU.is_ge))
                link(dve.tensor_reduce(eid_f[:], passed[:], AX_X, ALU.add))
                if f == 1:
                    dve.wait_ge(exp_done, NS)
                dve.tensor_scalar(eid[:], eid_f[:], float(E - 1), None, ALU.min).then_inc(eid_made, 1)
                dve.wait_ge(list_done, f + 1)
                link(dve.tensor_copy(tok_lo[:], list_ps[:, 0:NS]))
                dve.scalar_tensor_tensor(out=tok[:], in0=list_ps[:, NS:2 * NS], scalar=float(P),
                                         in1=tok_lo[:], op0=ALU.mult, op1=ALU.add).then_inc(tok_made, 1)

            def experts(f):
                def tile(t, t_mod, done, used):
                    e = dve.value_load(eid[0:1, bass.ds(t, 1)], min_val=0, max_val=E - 1)
                    dve.wait_ge(exp_done, done)
                    if used is not None:
                        dve.wait_ge(yrow_made, used)
                    dve.tensor_tensor(ypre[:, t_mod % 2, :], y_ps[t_mod % 2][:],
                                      be_bc[:, bass.ds(e * H, H)], ALU.add).then_inc(ypre_made, 1)

                dve.wait_ge(eid_made, f + 1)
                for t in range(2):
                    used = f * NS + t - 1
                    tile(t, t, f * NS + t + 1, used if used > 0 else None)
                loops = (NS - 3) // 2
                with dve.Fori(0, loops) as r:
                    for j in range(2):
                        t = 2 + j
                        tile(r * 2 + t, t, r * 2 + (f * NS + t + 1), r * 2 + (f * NS + t - 1))
                for t in range(2 + 2 * loops, NS):
                    tile(t, t, f * NS + t + 1, f * NS + t - 1)

            def add_back(f, i):
                for k in range(TOP_K):
                    m = (f * NT + i) * TOP_K + k
                    dve.wait_ge(back[m % CG], 16 * (m // CG + 1))
                    ins = dve.tensor_tensor(x[:, i, :], x[:, i, :], cg[:, m % CG, :], ALU.add)
                    if k < TOP_K - 1:
                        link(ins)
                    else:
                        ins.then_inc(x_ffn, 1)
                dve.wait_ge(x_ffn, f * NT + i + 1)

            def add_bv(b):
                dve.wait_ge(v_done, b + 1)
                if b >= 2:
                    dve.wait_ge(ot_done, b - 1)
                dve.tensor_tensor(v_ring[b % 2][:], vo_ps[:, 0:TB * D].rearrange("p (t d) -> p t d", t=TB),
                                  bv_bc[:].unsqueeze(1).broadcast_to([P, TB, D]), ALU.add
                                  ).then_inc(v_made, 1)

            dve.wait_ge(const_made, 9)
            dve.wait_ge(x_in_sem[0], 16)
            moments("g0", 0)
            for i in range(NT):
                if i % TB == 0 and i // TB + 1 < B:
                    dve.wait_ge(x_in_sem[i // TB + 1], 16)
                    moments("g0", i // TB + 1)
                normalise("g0", i)
                if i == 1:
                    dve.wait_ge(small_in, 16 * SMALL)
                if i >= 1:
                    choose(0, i - 1)
            choose(0, NT - 1)
            route(0)
            experts(0)
            for i in range(TB):
                add_back(0, i)
            moments("att", 0)
            for i in range(TB):
                normalise("att", i)
            add_bv(0)
            for b in range(B):
                dve.wait_ge(score_done, b + 1)
                if b:
                    dve.wait_ge(prob_made, TB * b)
                link(dve.tensor_reduce(smax[:], sp_ps[:].rearrange("p (q k) -> p q k", q=TB), AX_X, ALU.max))
                dve.tensor_scalar(nmax[:], smax[:], -SCALE, None, ALU.mult).then_inc(nmax_made, 1)
                if b + 1 < B:
                    for i in range(TB * (b + 1), TB * (b + 2)):
                        add_back(0, i)
                    moments("att", b + 1)
                    for i in range(TB * (b + 1), TB * (b + 2)):
                        normalise("att", i)
                if b >= 1:
                    for i in range(TB * (b - 1), TB * b):
                        choose(1, i)
                if b + 1 < B:
                    add_bv(b + 1)
                dve.wait_ge(prob_made, TB * (b + 1))
                link(dve.reciprocal(pinv[:], psumrow[:]))
                for q in range(TB):
                    i = TB * b + q
                    dve.wait_ge(bo_added, i + 1)
                    dve.wait_ge(wo_done, i + 1)
                    ins = dve.scalar_tensor_tensor(out=x[:, i, :], in0=y0_ps[:], scalar=pinv[:, q:q + 1],
                                                   in1=x[:, i, :], op0=ALU.mult, op1=ALU.add)
                    ins.then_inc(x_att, 1)
                    dve.wait_ge(x_att, i + 1)
                moments("g1", b)
                for i in range(TB * b, TB * (b + 1)):
                    normalise("g1", i)
            for i in range(TB * (B - 1), NT):
                choose(1, i)
            route(1)
            experts(1)
            for i in range(NT):
                add_back(1, i)


_INS = ['L0_attn_x', 'L0_attn_Wqkv', 'L0_attn_bqkv', 'L0_attn_Wo', 'L0_attn_bo',
        'L0_ffn_W_gate', 'L0_ffn_b_gate', 'L0_ffn_W_e', 'L0_ffn_b_e']


def kernel(**inputs):
    import numpy as _np
    import concourse.bacc as _bacc
    from concourse import mybir as _mybir
    from concourse.bass_utils import run_bass_kernel_spmd as _run

    nc = _bacc.Bacc("TRN2", target_bir_lowering=False, num_devices=1)
    arrays, args = {}, []
    for name in _INS:
        a = _np.ascontiguousarray(inputs[name])
        arrays[f"in_{name}_dram"] = a
        args.append(nc.dram_tensor(f"in_{name}_dram", a.shape, _mybir.dt.from_np(a.dtype),
                                   kind="ExternalInput").ap())
    out = nc.dram_tensor("out_0_dram", inputs['L0_attn_x'].shape, _mybir.dt.float32,
                         kind="ExternalOutput").ap()
    macaron_kernel(nc, *args, out)
    r = _run(nc, [arrays], core_ids=[0])
    return r.results[0]["out_0_dram"]
```

```python
from contextlib import ExitStack

import concourse.bass as bass
from concourse import mybir

P = 128
ALU = mybir.AluOpType
ACT = mybir.ActivationFunctionType
F32 = mybir.dt.float32
F32R = mybir.dt.float32r
BF16 = mybir.dt.bfloat16
I32 = mybir.dt.int32
U32 = mybir.dt.uint32
AX_X = mybir.AxisListType.X
EPS = 1e-5
TOP_K = 2


def macaron_kernel(nc, x_in, w_qkv, b_qkv, w_o, b_o, w_gate, b_gate, w_e, b_e, out):
    B, S, H = x_in.shape
    E, _, HO = w_e.shape
    D = w_o.shape[0]
    T = B * S
    NT = T // P
    NC = H // P
    TB = S // P
    J = NT * TOP_K
    JB = TB * TOP_K
    NS = T * TOP_K // P + E - 1
    WE = NC * H
    SCALE = float(D) ** -0.5
    HALF_MEAN = 0.5 / TOP_K
    NO_PAIR = 2 * TOP_K * T
    assert S == 2 * P and D == P and HO == H and H == 512 and NT <= 8 and NT % 2 == 0
    assert T & (T - 1) == 0

    x_rows = x_in.rearrange("b s h -> (b s) h")
    out_rows = out.rearrange("b s h -> (b s) h")

    with ExitStack() as ctx:
        def sb(name, shape, dt=F32, at=ctx):
            return at.enter_context(nc.sbuf_tensor(name, shape, dt))

        def psum(name, shape):
            return ctx.enter_context(nc.psum_tensor(name, shape, F32))

        def sem(name):
            return ctx.enter_context(nc.semaphore(name))

        xn_dram = [nc.dram_tensor(f"xn_dram{f}", [T, H], F32, kind="Internal") for f in range(2)]
        z_dram = [nc.dram_tensor(f"z_dram{f}", [TOP_K * T, H], F32, kind="Internal") for f in range(2)]

        XN = 4
        XG = 4
        YB = 4
        ZB = 2
        ZT = 6
        MR = 8
        x = sb("x", [P, NT, H])
        whi = sb("whi", [P, E * WE], F32R)
        with ExitStack() as loading:
            raw = sb("raw", [P, E * WE], at=loading)
        wlo = sb("wlo", [P, E * WE], F32R)
        be_bc = sb("be_bc", [P, E * H])
        wqkv = sb("wqkv", [P, NC, 3 * D])
        wo = sb("wo", [P, H])
        wg = sb("wg", [P, NC, E])
        bg = sb("bg", [E, 1])
        bo_bc = sb("bo_bc", [P, H])
        bv_bc = sb("bv_bc", [P, D])
        bqk = sb("bqk", [P, 2])
        stats = sb("stats", [P, MR, 6])
        mv = sb("mv", [P, MR, 2])
        var_eps = sb("var_eps", [P, MR])
        rstd = sb("rstd", [P, MR])
        neg_half = sb("neg_half", [P, TB])
        logit_t = sb("logit_t", [E, S])
        top = sb("top", [P, TB, 8])
        topi = sb("topi", [P, TB, 8], U32)
        topf = sb("topf", [P, TB, TOP_K])
        onehot = sb("onehot", [P, NT, TOP_K, E], BF16)
        ident = sb("ident", [P, P])
        before = sb("before", [P, P], BF16)
        ones = sb("ones", [P, P], BF16)
        ones_row = sb("ones_row", [1, P])
        iota_e = sb("iota_e", [P, E])
        iota_r = sb("iota_r", [P, P], BF16)
        iota_t = sb("iota_t", [P, NS])
        thresh = sb("thresh", [P, E, NT])
        place_id = sb("place_id", [P, 2, J])
        zeros_e = sb("zeros_e", [P, E])
        ntile = sb("ntile", [P, E])
        incl = sb("incl", [P, E])
        excl = sb("excl", [P, E])
        rank_f = sb("rank_f", [P, J])
        rank_u = sb("rank_u", [P, J], U32)
        slot_r = sb("slot_r", [P, J], U32)
        rank_t = sb("rank_t", [P, J], U32)
        start_t = sb("start_t", [P, J])
        slot_t = sb("slot_t", [P, J])
        place_lo = sb("place_lo", [P, NS])
        place = sb("place", [P, NS], U32)
        tok = sb("tok", [P, NS], U32)
        eid_f = sb("eid_f", [1, NS])
        eid = sb("eid", [1, NS], I32)
        nmax = sb("nmax", [P, TB])
        smax = sb("smax", [P, TB])
        psumrow = sb("psumrow", [P, TB])
        pinv = sb("pinv", [P, TB])

        with ExitStack() as shared:
            xn = sb("xn", [P, XN, H], at=shared)
            xt_gate = sb("xt_gate", [P, NC, S], at=shared)
            with ExitStack() as part:
                picked = sb("picked", [P, NT, TOP_K, E], at=part)
                row_hot = sb("row_hot", [P, J, P], BF16, at=part)
                mark = sb("mark", [P, 2, J, NS], BF16, at=part)
                above = sb("above", [P, E, NT], at=part)
                in_tile = sb("in_tile", [P, J, NS], at=part)
                passed = sb("passed", [1, NS, E], at=part)
                xn_more = sb("xn_more", [P, NT - XN, H], at=part)
            with ExitStack() as part:
                z_att = sb("z_att", [P, ZB, TOP_K, H], at=part)
                xt_att = sb("xt_att", [P, NC, S], at=part)
                qk = sb("qk", [P, 2, S], at=part)
                v_ring = [sb(f"v{i}", [P, TB, D], at=part) for i in range(2)]
                prob = sb("prob", [P, TB, S], at=part)
                pt = sb("pt", [P, TB, S], at=part)
                ot = prob[:, 0, :]
        with ExitStack() as shared:
            xg = sb("xg", [P, XG, H], at=shared)
            xt_hi = sb("xt_hi", [P, 2, H], F32R, at=shared)
            xt_lo = sb("xt_lo", [P, 2, H], F32R, at=shared)
            ypre = sb("ypre", [P, 2, H], at=shared)
            yrow = sb("yrow", [P, YB, H], at=shared)
        with ExitStack() as shared:
            z_end = sb("z_end", [P, ZT, TOP_K, H], at=shared)
        ZR = [z_att, z_end]

        tp_ps = [psum(f"tp_ps{i}", [P, 512]) for i in range(2)]
        y0_ps = psum("y0_ps", [P, 512])
        qk_ps = psum("qk_ps", [P, 512])
        v_ps = psum("v_ps", [P, 512])
        sp_ps = psum("sp_ps", [P, 512])
        g_ps = psum("g_ps", [P, 512])
        rk_ps = psum("rk_ps", [P, 512])
        y_ps = [y0_ps, qk_ps]
        be_ps = [y0_ps, qk_ps, v_ps, sp_ps]
        gate_ps = g_ps[0:E, 0:S]
        logit_ps = g_ps[:, S:S + TB * E].rearrange("p (t e) -> p t e", e=E)
        rank = rk_ps[:, 0:(NT + 1) * E].rearrange("p (t e) -> p t e", e=E)
        list_ps = g_ps[:, 0:2 * NS].rearrange("p (a t) -> p a t", a=2)

        CONSTS = 11
        ATT_LOADS = 5
        x_in_sem = [sem(f"x_loaded{b}") for b in range(B)]
        gate_in = sem("gate_weights_loaded")
        be_in = sem("be_loaded")
        raw_in = [sem(f"raw_loaded{n}") for n in range(2 * E)]
        att_in = sem("attention_weights_loaded")
        const_made = sem("const_made")
        const_step = sem("const_step")
        be_done = sem("be_done")
        be_copied = sem("be_copied")
        be_copied_act = sem("be_copied_act")
        hi_made = sem("hi_made")
        lo_made_dve = sem("lo_made_dve")
        lo_made_pool = sem("lo_made_pool")
        dve_step = sem("dve_step")
        var_made = sem("var_made")
        rstd_made = sem("rstd_made")
        xn_made = sem("xn_made")
        xn_stored = [sem(f"xn_stored{s}") for s in range(NT)]
        tp_full = sem("tp_full")
        tp_copied = sem("tp_copied")
        gate_done = sem("gate_done")
        gate_copied = sem("gate_copied")
        logit_done = sem("logit_done")
        logit_read = sem("logit_read")
        onehot_made = sem("onehot_made")
        rank_done = sem("rank_done")
        rank_read = sem("rank_read")
        mark_made = sem("mark_made")
        row_made = sem("row_made")
        row_hot_made = sem("row_hot_made")
        list_done = sem("list_done")
        tok_made = sem("tok_made")
        eid_made = sem("eid_made")
        gathered = [sem(f"gathered{s}") for s in range(XG)]
        xt_made = sem("xt_made")
        exp_done = sem("exp_done")
        ypre_made = sem("ypre_made")
        yrow_made = sem("yrow_made")
        scattered = [sem(f"scattered{s}") for s in range(YB)]
        z_in = [[sem(f"z_loaded{f}_{s}") for s in range((ZB, ZT)[f])] for f in range(2)]
        z_summed = sem("z_summed")
        x_ffn = sem("x_ffn")
        bo_added = sem("bo_added")
        qk_done = sem("qk_done")
        qk_copied = sem("qk_copied")
        v_done = sem("v_done")
        v_made = sem("v_made")
        score_done = sem("score_done")
        nmax_made = sem("nmax_made")
        prob_made = sem("prob_made")
        pt_done = sem("pt_done")
        pt_copied = sem("pt_copied")
        ot_done = sem("ot_done")
        ot_copied = sem("ot_copied")
        wo_done = sem("wo_done")
        x_att = sem("x_att")
        out_stored = sem("out_stored")

        def of(kind, b):
            return [(kind, i) for i in range(TB * b, TB * (b + 1))]

        uses = [u for b in range(B) for u in of("g0", b)] + [("exp0", t) for t in range(NS)]
        uses += of("att", 0)
        norms = [u for b in range(B) for u in of("g0", b)] + of("att", 0) + of("att", 1)
        for b in range(B):
            uses += (of("att", b + 1) if b + 1 < B else []) + (of("g1", b - 1) if b else [])
            norms += (of("att", b + 2) if b + 2 < B else []) + of("g1", b)
        uses += of("g1", B - 1) + [("exp1", t) for t in range(NS)]
        use_no = {u: n for n, u in enumerate(uses)}
        norm_no = {u: n for n, u in enumerate(norms)}

        def xn_slot(n):
            return n if n < NT else n % XN

        def xn_at(n):
            s = xn_slot(n)
            return xn[:, s, :] if s < XN else xn_more[:, s - XN, :]

        def last_in_slot(n):
            return next((m for m in range(n - 1, -1, -1) if xn_slot(m) == xn_slot(n)), None)

        def stores_from(s, upto):
            return sum(1 for n in range(upto) if xn_slot(n) == s and norms[n][0] != "att")

        WARM_ATT = 12
        WARM = 20
        AHEAD = 5
        DVE_HALVES = [1, 3, 5, 11, 12, 13, 14, 15]
        POOL_HALVES = [n for n in range(2 * E) if n not in DVE_HALVES]

        BE_ACT = [E - 2, E - 1]

        def half(w, n):
            return w[:, n * (WE // 2):(n + 1) * (WE // 2)]

        def split_lo(eng, n, done):
            eng.wait_ge(hi_made, n + 1)
            eng.tensor_tensor(half(wlo, n), half(raw, n), half(whi, n).bitcast(F32),
                              ALU.subtract).then_inc(done, 1)

        HEAD, STEP = 2, 4
        LOOPS = (NS - 1 - HEAD) // STEP
        REST = HEAD + LOOPS * STEP

        def slot_uses(ring, s):
            return sum(1 for t in range(NS) if t % ring == s)

        block = ctx.enter_context(nc.Block())

        @block.sync
        def _(sp):
            for b in range(B):
                sp.dma_start(x[:, TB * b:TB * (b + 1), :],
                             x_rows[b * S:(b + 1) * S, :].rearrange("(t p) h -> p t h", p=P)
                             ).then_inc(x_in_sem[b], 16)
            for n in range(2 * E):
                if n >= AHEAD:
                    sp.wait_ge(hi_made, n - AHEAD + 1)
                rows = w_e[n // 2].rearrange("(c p) h -> p c h", p=P)
                sp.dma_start(half(raw, n).rearrange("p (c h) -> p c h", h=H),
                             rows[:, NC // 2 * (n % 2):NC // 2 * (n % 2 + 1), :]
                             ).then_inc(raw_in[n], 16)
            sp.dma_start(wqkv[:], w_qkv.rearrange("(c p) n -> p c n", p=P)).then_inc(att_in, 16)
            sp.dma_start(wo[:], w_o).then_inc(att_in, 16)

            def load_z(f, i):
                ring = (ZB, ZT)[f]
                if i == 0:
                    for s in range(YB):
                        sp.wait_ge(scattered[s], 16 * (f + 1) * slot_uses(YB, s))
                if i >= ring:
                    sp.wait_ge(x_ffn, f * NT + i - ring + 1)
                sp.dma_start(ZR[f][:, i % ring, :, :],
                             z_dram[f].rearrange("(k t p) h -> t p k h", k=TOP_K, p=P)[i]
                             ).then_inc(z_in[f][i % ring], 16)

            for i in range(NT):
                load_z(0, i)
            for i in range(min(ZT, NT)):
                load_z(1, i)
            for i in range(NT):
                sp.wait_ge(x_ffn, NT + i + 1)
                sp.dma_start(out_rows[i * P:(i + 1) * P, :], x[:, i, :]).then_inc(out_stored, 16)
                if i + ZT < NT:
                    load_z(1, i + ZT)
            sp.wait_ge(out_stored, 16 * NT)

        @block.gpsimd
        def _(pool):
            steps = [0]

            def link(ins):
                steps[0] += 1
                ins.then_inc(const_step, 1)
                pool.wait_ge(const_step, steps[0])

            pool.memset(ones_row[:], 1.0).then_inc(const_made, 1)
            link(pool.memset(ident[:], 0.0))
            pool.affine_select(out=ident[:], in_=ident[:], compare_op=ALU.not_equal, fill=1.0, base=0,
                               pattern=[[-1, P]], channel_multiplier=1).then_inc(const_made, 1)
            pool.memset(neg_half[:], -0.5).then_inc(const_made, 1)
            pool.iota(iota_e[:], pattern=[[1, E]], base=0, channel_multiplier=0,
                      allow_small_or_imprecise_dtypes=True).then_inc(const_made, 1)
            link(pool.memset(ones[:], 1.0))
            pool.affine_select(out=before[:], in_=ones[:], compare_op=ALU.is_gt, fill=0.0, base=0,
                               pattern=[[1, P]], channel_multiplier=-1).then_inc(const_made, 1)
            pool.iota(iota_r[:], pattern=[[1, P]], base=0, channel_multiplier=0,
                      allow_small_or_imprecise_dtypes=True).then_inc(const_made, 1)
            pool.iota(iota_t[:], pattern=[[1, NS]], base=0, channel_multiplier=0,
                      allow_small_or_imprecise_dtypes=True).then_inc(const_made, 1)
            pool.iota(thresh[:], pattern=[[0, E], [P, NT]], base=0, channel_multiplier=0,
                      allow_small_or_imprecise_dtypes=True).then_inc(const_made, 1)
            pool.iota(place_id[:, 0, :], pattern=[[0, J]], base=0, channel_multiplier=1,
                      allow_small_or_imprecise_dtypes=True).then_inc(const_made, 1)
            pool.iota(place_id[:, 1, :].rearrange("p (t k) -> p t k", k=TOP_K), pattern=[[P, NT], [T, TOP_K]],
                      base=-NO_PAIR, channel_multiplier=0,
                      allow_small_or_imprecise_dtypes=True).then_inc(const_made, 1)
            pool.memset(zeros_e[:], 0.0).then_inc(const_made, 1)

            def deviations(kind, b):
                n = norm_no[(kind, TB * b)]
                s = n % MR
                pool.wait_ge(var_made, n // TB + 1)
                if n >= MR:
                    pool.wait_ge(xn_made, n - MR + TB)
                pool.tensor_tensor(rstd[:, s:s + TB], var_eps[:, s:s + TB], neg_half[:], ALU.pow
                                   ).then_inc(rstd_made, 1)

            def gather(f, t):
                if t >= XG:
                    pool.wait_ge(tp_full, use_no[(f"exp{f}", t - XG)] + 1)
                pool.indirect_dma_start(
                    out=xg[:, t % XG, :], out_offset=None, in_=xn_dram[f][:, :],
                    in_offset=bass.IndirectOffsetOnAxis(ap=tok[:, t:t + 1], axis=0)
                ).then_inc(gathered[t % XG], 16)

            def scatter(f, t):
                pool.wait_ge(yrow_made, f * NS + t + 1)
                pool.indirect_dma_start(
                    out=z_dram[f][:, :], out_offset=bass.IndirectOffsetOnAxis(ap=place[:, t:t + 1], axis=0),
                    in_=yrow[:, t % YB, :], in_offset=None, bounds_check=TOP_K * T - 1, oob_is_err=False
                ).then_inc(scattered[t % YB], 16)

            def experts(f):
                pool.wait_ge(tok_made, f + 1)
                for s in range(NT):
                    pool.wait_ge(xn_stored[s], 16 * stores_from(s, len(norms) if f else NT))
                for t in range(XG):
                    gather(f, t)
                for t in range(NS):
                    if t + XG < NS:
                        gather(f, t + XG)
                    scatter(f, t)

            def sum_z(i):
                pool.wait_ge(z_in[0][i % ZB], 16 * (i // ZB + 1))
                z = ZR[0][:, i % ZB, :, :]
                pool.tensor_tensor(z[:, 0, :], z[:, 0, :], z[:, 1, :], ALU.add).then_inc(z_summed, 1)

            def add_bo(b):
                for i in range(TB * b, TB * (b + 1)):
                    pool.wait_ge(xn_made, norm_no[("att", i)] + 1)
                    pool.tensor_tensor(x[:, i, :], x[:, i, :], bo_bc[:], ALU.add).then_inc(bo_added, 1)

            def attention_input(b):
                for i in range(TB * b, TB * (b + 1)):
                    sum_z(i)
                deviations("att", b)

            for b in range(B):
                deviations("g0", b)
            for n in POOL_HALVES:
                split_lo(pool, n, lo_made_pool)
            experts(0)
            pool.wait_ge(att_in, 16 * ATT_LOADS)
            attention_input(0)
            attention_input(1)
            add_bo(0)
            add_bo(1)
            for b in range(B):
                if b + 2 < B:
                    attention_input(b + 2)
                    add_bo(b + 2)
                deviations("g1", b)
            experts(1)

        @block.scalar
        def _(act):
            act.dma_start(be_bc[0:1, :], b_e.rearrange("(a e) h -> a (e h)", a=1)).then_inc(be_in, 16)
            act.dma_start(wg[:], w_gate.rearrange("(c p) e -> p c e", p=P)).then_inc(gate_in, 16)
            act.dma_start(bg[:], b_gate.rearrange("(e a) -> e a", a=1),
                          allow_slow_non_contiguous=True).then_inc(gate_in, 16)

            def split_hi(n):
                act.wait_ge(raw_in[n], 16)
                act.activation(half(whi, n), half(raw, n), ACT.Copy).then_inc(hi_made, 1)

            def store_xn(f, i):
                m = norm_no[(f"g{f}", i)]
                act.wait_ge(xn_made, m + 1)
                act.dma_start(xn_dram[f][i * P:(i + 1) * P, :], xn_at(m)
                              ).then_inc(xn_stored[xn_slot(m)], 16)

            def copy_gate(f, b):
                for i in range(TB * b, TB * (b + 1)):
                    n = use_no[(f"g{f}", i)]
                    store_xn(f, i)
                    if f * B + b:
                        act.wait_ge(gate_done, f * B + b)
                    act.wait_ge(tp_full, n + 1)
                    act.activation(xt_gate[:, :, (i % TB) * P:(i % TB + 1) * P],
                                   tp_ps[n % 2][:].rearrange("p (c t) -> p c t", c=NC),
                                   ACT.Copy).then_inc(tp_copied, 1)

            def copy_logits(f, b):
                m = f * B + b
                act.wait_ge(gate_done, m + 1)
                if m:
                    act.wait_ge(logit_done, m)
                act.activation(logit_t[:], gate_ps, ACT.Identity, bias=bg[:]).then_inc(gate_copied, 1)

            def copy_att(b):
                for i in range(TB * b, TB * (b + 1)):
                    n = use_no[("att", i)]
                    if b:
                        act.wait_ge(v_done, b)
                    act.wait_ge(tp_full, n + 1)
                    act.activation(xt_att[:, :, (i % TB) * P:(i % TB + 1) * P],
                                   tp_ps[n % 2][:].rearrange("p (c t) -> p c t", c=NC),
                                   ACT.Copy).then_inc(tp_copied, 1)

            def experts(f):
                n0 = use_no[(f"exp{f}", 0)]

                def hi_rows(t, full, done):
                    act.wait_ge(tp_full, full)
                    if done is not None:
                        act.wait_ge(exp_done, done)
                    act.activation(xt_hi[:, t % 2, :], tp_ps[(n0 + t) % 2][:], ACT.Copy
                                   ).then_inc(tp_copied, 1)

                def relu(t, made, sent):
                    act.wait_ge(ypre_made, made)
                    if sent is not None:
                        act.wait_ge(scattered[t % YB], sent)
                    act.activation(yrow[:, t % YB, :], ypre[:, t % 2, :], ACT.Relu,
                                   scale=HALF_MEAN).then_inc(yrow_made, 1)

                def sent(t):
                    return 16 * (f * slot_uses(YB, t % YB) + t // YB)

                def tile(t):
                    if t + 1 < NS:
                        hi_rows(t + 1, n0 + t + 2, f * NS + t or None)
                    relu(t, f * NS + t + 1, sent(t) or None)

                hi_rows(0, n0 + 1, None)
                for t in range(HEAD + STEP):
                    tile(t)
                with act.Fori(1, LOOPS) as r:
                    for j in range(STEP):
                        t = HEAD + j
                        hi_rows(t + 1, r * STEP + (n0 + t + 2), r * STEP + (f * NS + t))
                        relu(t, r * STEP + (f * NS + t + 1), r * (16 * STEP // YB) + sent(t))
                for t in range(REST, NS):
                    tile(t)

            def copy_qk(b):
                act.wait_ge(qk_done, b + 1)
                if b:
                    act.wait_ge(score_done, b)
                for j in range(2):
                    act.activation(qk[:, j, :], qk_ps[:, j * S:(j + 1) * S], ACT.Identity,
                                   bias=bqk[:, j:j + 1]).then_inc(qk_copied, 1)

            def softmax(b):
                act.wait_ge(nmax_made, b + 1)
                if b:
                    act.wait_ge(wo_done, TB * b)
                    act.wait_ge(x_att, TB * b)
                for q in range(TB):
                    act.activation(prob[:, q, :], sp_ps[:, q * S:(q + 1) * S], ACT.Exp,
                                   bias=nmax[:, q:q + 1], scale=SCALE,
                                   accum_out=psumrow[:, q:q + 1]).then_inc(prob_made, 1)

            act.wait_ge(gate_in, 32)
            for b in range(B):
                if b:
                    copy_logits(0, b - 1)
                copy_gate(0, b)
                for n in range(2 * b, 2 * b + 2):
                    split_hi(n)
            copy_logits(0, B - 1)
            for n in range(2 * B, 2 * E):
                split_hi(n)
            for e in BE_ACT:
                act.wait_ge(be_done, e + 1)
                act.activation(be_bc[:, e * H:(e + 1) * H], be_ps[e % len(be_ps)][:], ACT.Copy
                               ).then_inc(be_copied_act, 1)
            act.dma_start(bqk[:], b_qkv[0:2 * D].rearrange("(j d) -> d j", j=2),
                          allow_slow_non_contiguous=True).then_inc(att_in, 16)
            act.dma_start(bv_bc[:], b_qkv[2 * D:3 * D].partition_broadcast(P)).then_inc(att_in, 16)
            act.dma_start(bo_bc[:], b_o.partition_broadcast(P)).then_inc(att_in, 16)
            experts(0)
            act.wait_ge(att_in, 16 * ATT_LOADS)
            copy_att(0)
            copy_qk(0)
            for b in range(B):
                if b + 1 < B:
                    copy_att(b + 1)
                softmax(b)
                if b + 1 < B:
                    copy_qk(b + 1)
                act.wait_ge(pt_done, b + 1)
                if b:
                    act.wait_ge(ot_done, b)
                act.activation(pt[:].rearrange("p t s -> p (t s)"), sp_ps[:], ACT.Copy
                               ).then_inc(pt_copied, 1)
                act.wait_ge(ot_done, b + 1)
                act.activation(ot, sp_ps[:, 0:S], ACT.Copy).then_inc(ot_copied, 1)
                if b:
                    copy_gate(1, b - 1)
                    copy_logits(1, b - 1)
            copy_gate(1, B - 1)
            copy_logits(1, B - 1)
            experts(1)

        @block.tensor
        def _(pe):
            def warm_up(n):
                for _ in range(n):
                    pe.matmul(rk_ps[:], ones[:], ones[:].unsqueeze(1).broadcast_to([P, 4, P]),
                              start=True, stop=True)

            def broadcast_be(e):
                if e >= len(be_ps):
                    pe.wait_ge(be_copied, e - len(be_ps) + 1)
                pe.matmul(be_ps[e % len(be_ps)][:], ones_row[:], be_bc[0:1, e * H:(e + 1) * H],
                          start=True, stop=True).then_inc(be_done, 1)

            def transpose_xn(kind, b):
                for i in range(TB * b, TB * (b + 1)):
                    n, m = use_no[(kind, i)], norm_no[(kind, i)]
                    pe.wait_ge(xn_made, m + 1)
                    if n >= 2:
                        if n - 2 in exp_uses:
                            pe.wait_ge(xt_made, exp_uses[n - 2] + 1)
                        else:
                            pe.wait_ge(tp_copied, n - 1)
                    for c in range(NC):
                        last = pe.transpose(tp_ps[n % 2][:, c * P:(c + 1) * P],
                                            xn_at(m)[:, c * P:(c + 1) * P], ident[:])
                    last.then_inc(tp_full, 1)

            exp_uses = {n: int(kind[-1]) * NS + t for n, (kind, t) in enumerate(uses) if kind[:3] == "exp"}

            def gate(f, b):
                pe.wait_ge(tp_copied, use_no[(f"g{f}", TB * (b + 1) - 1)] + 1)
                if f * B + b:
                    pe.wait_ge(logit_read, f * B + b)
                for c in range(NC):
                    last = pe.matmul(gate_ps, wg[:, c, :], xt_gate[:, c, :],
                                     start=(c == 0), stop=(c == NC - 1))
                last.then_inc(gate_done, 1)

            def transpose_logits(f, b):
                pe.wait_ge(gate_copied, f * B + b + 1)
                for i in range(TB):
                    last = pe.transpose(logit_ps[:, i, :], logit_t[:, i * P:(i + 1) * P], ident[0:E, 0:E])
                last.then_inc(logit_done, 1)

            def count(f, b):
                pe.wait_ge(onehot_made, f * B + b + 1)
                if b:
                    pe.wait_ge(rank_read, f * (B + 1) + b)
                elif f:
                    pe.wait_ge(rank_read, B + 1)
                for i in range(TB * b, TB * (b + 1)):
                    for k in range(TOP_K):
                        pe.matmul(rank[:, i, :], before[:], onehot[:, i, k, :],
                                  start=(i == 0 and k == 0), stop=False, skip_group_check=True)
                        rest = onehot[:, i, k, :].unsqueeze(1).broadcast_to([P, NT - i, E])
                        last = pe.matmul(rank[:, i + 1:NT + 1, :], ones[:], rest,
                                         start=False, stop=(i == NT - 1 and k == TOP_K - 1),
                                         skip_group_check=True)
                last.then_inc(rank_done, 1)

            def token_list(f):
                for j in range(J):
                    if j % (J // 2) == 0:
                        pe.wait_ge(mark_made, 2 * f + j // (J // 2) + 1)
                    if j % JB == 0:
                        pe.wait_ge(row_hot_made, (f * J + j) // JB + 1)
                    last = pe.matmul(list_ps, row_hot[:, j, :], mark[:, :, j, :],
                                     start=(j == 0), stop=(j == J - 1))
                last.then_inc(list_done, 1)
                warm_up(WARM)

            def experts(f):
                n0 = use_no[(f"exp{f}", 0)]

                def transposes(t, landed, free_sem, free):
                    pe.wait_ge(gathered[t % XG], landed)
                    pe.wait_ge(free_sem, free)
                    for c in range(NC):
                        last = pe.transpose(tp_ps[(n0 + t) % 2][:, c * P:(c + 1) * P],
                                            xg[:, t % XG, c * P:(c + 1) * P], ident[:])
                    last.then_inc(tp_full, 1)

                def product(t, tile_no, made, read):
                    e = pe.value_load(eid[0:1, bass.ds(tile_no, 1)], min_val=0, max_val=E - 1)
                    pe.wait_ge(xt_made, made)
                    if read is not None:
                        pe.wait_ge(ypre_made, read)
                    n = 0
                    for rows, w in ((xt_hi, whi), (xt_hi, wlo), (xt_lo, whi)):
                        for c in range(NC):
                            last = pe.matmul(y_ps[t % 2][:], rows[:, t % 2, c * P:(c + 1) * P],
                                             w[:, bass.ds(e * WE + c * H, H)],
                                             start=(n == 0), stop=(n == 3 * NC - 1))
                            n += 1
                    last.then_inc(exp_done, 1)

                def landed(t):
                    return 16 * (f * slot_uses(XG, t % XG) + t // XG + 1)

                def tile(t):
                    if t + 1 < NS:
                        if t:
                            transposes(t + 1, landed(t + 1), xt_made, f * NS + t)
                        else:
                            transposes(t + 1, landed(t + 1), tp_copied, n0)
                    product(t, t, f * NS + t + 1, f * NS + t - 1 if f or t >= 2 else None)

                transposes(0, landed(0), tp_copied, n0 - 1)
                pe.wait_ge(eid_made, f + 1)
                if f == 0:
                    pe.wait_ge(lo_made_dve, len(DVE_HALVES))
                    pe.wait_ge(lo_made_pool, len(POOL_HALVES))
                    pe.wait_ge(be_copied, E - len(BE_ACT))
                    pe.wait_ge(be_copied_act, len(BE_ACT))
                for t in range(HEAD):
                    tile(t)
                with pe.Fori(0, LOOPS) as r:
                    for j in range(STEP):
                        t = HEAD + j
                        transposes(t + 1, r * (16 * STEP // XG) + landed(t + 1), xt_made,
                                   r * STEP + (f * NS + t))
                        product(t, r * STEP + t, r * STEP + (f * NS + t + 1), r * STEP + (f * NS + t - 1))
                for t in range(REST, NS):
                    tile(t)

            def project_qk(b):
                pe.wait_ge(tp_copied, use_no[("att", TB * (b + 1) - 1)] + 1)
                if b:
                    pe.wait_ge(qk_copied, 2 * b)
                else:
                    pe.wait_ge(ypre_made, NS)
                if b >= 2:
                    pe.wait_ge(x_att, TB * (b - 1))
                for j in range(2):
                    for c in range(NC):
                        last = pe.matmul(qk_ps[:, j * S:(j + 1) * S], wqkv[:, c, j * D:(j + 1) * D],
                                         xt_att[:, c, :], start=(c == 0), stop=(c == NC - 1))
                last.then_inc(qk_done, 1)

            def project_v(b):
                if b:
                    pe.wait_ge(v_made, b)
                for i in range(TB):
                    for c in range(NC):
                        last = pe.matmul(v_ps[:, i * D:(i + 1) * D], xt_att[:, c, i * P:(i + 1) * P],
                                         wqkv[:, c, 2 * D:3 * D], start=(c == 0), stop=(c == NC - 1))
                last.then_inc(v_done, 1)

            def scores(b):
                pe.wait_ge(qk_copied, 2 * (b + 1))
                if b:
                    pe.wait_ge(ot_copied, b)
                for q in range(TB):
                    last = pe.matmul(sp_ps[:, q * S:(q + 1) * S], qk[:, 0, q * P:(q + 1) * P],
                                     qk[:, 1, :], start=True, stop=True)
                last.then_inc(score_done, 1)

            def transpose_prob(b):
                pe.wait_ge(prob_made, TB * (b + 1))
                for k in range(TB):
                    for q in range(TB):
                        last = pe.transpose(sp_ps[:, k * S + q * P:k * S + (q + 1) * P],
                                            prob[:, q, k * P:(k + 1) * P], ident[:])
                last.then_inc(pt_done, 1)

            def mix_v(b):
                pe.wait_ge(pt_copied, b + 1)
                pe.wait_ge(v_made, b + 1)
                for k in range(TB):
                    last = pe.matmul(sp_ps[:, 0:S], v_ring[b % 2][:, k, :], pt[:, k, :],
                                     start=(k == 0), stop=(k == TB - 1))
                last.then_inc(ot_done, 1)

            def project_out(b):
                pe.wait_ge(ot_copied, b + 1)
                pe.wait_ge(qk_copied, 2 * min(b + 2, B))
                if b:
                    pe.wait_ge(x_att, TB * b)
                for q in range(TB):
                    pe.matmul(y_ps[q][:], ot[:, q * P:(q + 1) * P], wo[:], start=True, stop=True
                              ).then_inc(wo_done, 1)

            pe.wait_ge(const_made, CONSTS)
            warm_up(6)
            pe.wait_ge(be_in, 16)
            biases = list(range(E))
            for _ in range(2):
                broadcast_be(biases.pop(0))
            for b in range(B):
                transpose_xn("g0", b)
                if b:
                    transpose_logits(0, b - 1)
                broadcast_be(biases.pop(0))
                if b == 0:
                    pe.wait_ge(gate_in, 32)
                gate(0, b)
                if b:
                    count(0, b - 1)
            broadcast_be(biases.pop(0))
            transpose_logits(0, B - 1)
            count(0, B - 1)
            broadcast_be(biases.pop(0))
            token_list(0)
            experts(0)
            pe.wait_ge(z_in[0][0], 16)
            warm_up(WARM_ATT)
            pe.wait_ge(att_in, 16 * ATT_LOADS)
            transpose_xn("att", 0)
            project_qk(0)
            project_v(0)
            for b in range(B):
                scores(b)
                if b + 1 < B:
                    transpose_xn("att", b + 1)
                    project_qk(b + 1)
                if b >= 2:
                    transpose_logits(1, b - 2)
                transpose_prob(b)
                if b + 1 < B:
                    project_v(b + 1)
                mix_v(b)
                if b:
                    transpose_xn("g1", b - 1)
                project_out(b)
                if b >= 2:
                    count(1, b - 2)
                if b:
                    gate(1, b - 1)
            transpose_logits(1, B - 2)
            transpose_xn("g1", B - 1)
            count(1, B - 2)
            gate(1, B - 1)
            transpose_logits(1, B - 1)
            count(1, B - 1)
            token_list(1)
            experts(1)

        @block.vector
        def _(dve):
            steps = [0]

            def step(ins):
                steps[0] += 1
                ins.then_inc(dve_step, 1)
                return steps[0]

            def link(ins):
                dve.wait_ge(dve_step, step(ins))

            def copy_be(e):
                dve.wait_ge(be_done, e + 1)
                dve.tensor_copy(be_bc[:, e * H:(e + 1) * H], be_ps[e % len(be_ps)][:]).then_inc(be_copied, 1)

            def moments(kind, b):
                n = norm_no[(kind, TB * b)]
                s = n % MR
                read = [step(dve.bn_stats(stats[:, s + i, :], x[:, TB * b + i, :])) for i in range(TB)]
                for i in range(TB):
                    dve.wait_ge(dve_step, read[i])
                    last = step(dve.bn_aggr(mv[:, s + i, :], stats[:, s + i, :]))
                dve.wait_ge(dve_step, last)
                if n >= MR:
                    dve.wait_ge(rstd_made, (n - MR) // TB + 1)
                dve.tensor_scalar(var_eps[:, s:s + TB], mv[:, s:s + TB, 1], EPS, None,
                                  ALU.add).then_inc(var_made, 1)

            def normalise(kind, b):
                for i in range(TB * b, TB * (b + 1)):
                    n = norm_no[(kind, i)]
                    s = n % MR
                    if last_in_slot(n) is not None:
                        dve.wait_ge(tp_full, use_no[norms[last_in_slot(n)]] + 1)
                        if stores_from(xn_slot(n), n):
                            dve.wait_ge(xn_stored[xn_slot(n)], 16 * stores_from(xn_slot(n), n))
                    dve.wait_ge(rstd_made, n // TB + 1)
                    dve.tensor_scalar(xn_at(n), x[:, i, :], mv[:, s, 0:1], rstd[:, s:s + 1],
                                      ALU.subtract, ALU.mult).then_inc(xn_made, 1)

            def choose(f, b):
                m = f * B + b
                dve.wait_ge(logit_done, m + 1)
                tops = [step(dve.max(top[:, i, :], logit_ps[:, i, :])) for i in range(TB)]
                for i in range(TB):
                    dve.wait_ge(dve_step, tops[i])
                    last = dve.max_index(topi[:, i, :], top[:, i, :], logit_ps[:, i, :])
                    if i + 1 < TB:
                        step(last)
                last.then_inc(logit_read, 1)
                dve.wait_ge(logit_read, m + 1)
                link(dve.tensor_copy(topf[:], topi[:, :, 0:TOP_K]))
                dve.tensor_tensor(onehot[:, TB * b:TB * (b + 1), :, :],
                                  iota_e[:].unsqueeze(1).unsqueeze(1).broadcast_to([P, TB, TOP_K, E]),
                                  topf[:].unsqueeze(3).broadcast_to([P, TB, TOP_K, E]),
                                  ALU.is_equal).then_inc(onehot_made, 1)

            def pair_columns(b):
                return slice(JB * b, JB * (b + 1))

            def pick_rank(f, b):
                tiles = slice(TB * b, TB * (b + 1))
                dve.wait_ge(rank_done, f * B + b + 1)
                dve.tensor_tensor(picked[:, tiles], onehot[:, tiles],
                                  rank[:, tiles, :].unsqueeze(2).broadcast_to([P, TB, TOP_K, E]),
                                  ALU.mult).then_inc(rank_read, 1)

            def sum_rank(b):
                tiles = slice(TB * b, TB * (b + 1))
                return dve.tensor_reduce(rank_f[:, pair_columns(b)],
                                         picked[:, tiles].rearrange("p t k e -> p (t k) e"), AX_X, ALU.add)

            def rank_to_int(b):
                return dve.tensor_copy(rank_u[:, pair_columns(b)], rank_f[:, pair_columns(b)])

            def rank_row(b):
                return dve.tensor_single_scalar(slot_r[:, pair_columns(b)], rank_u[:, pair_columns(b)],
                                                P - 1, ALU.bitwise_and)

            def rank_tile(b):
                return dve.tensor_single_scalar(rank_t[:, pair_columns(b)], rank_u[:, pair_columns(b)],
                                                P.bit_length() - 1, ALU.logical_shift_right)

            def split_rank(f, b):
                pick_rank(f, b)
                dve.wait_ge(rank_read, f * (B + 1) + b + 1)
                link(sum_rank(b))
                link(rank_to_int(b))
                rank_row(b).then_inc(row_made, 1)
                step(rank_tile(b))

            def row_hots(f, b):
                dve.wait_ge(row_made, f * B + b + 1)
                dve.tensor_tensor(row_hot[:, pair_columns(b), :],
                                  iota_r[:].unsqueeze(1).broadcast_to([P, JB, P]),
                                  slot_r[:, pair_columns(b)].unsqueeze(2).broadcast_to([P, JB, P]),
                                  ALU.is_equal).then_inc(row_hot_made, 1)

            def route(f, halves_left):
                pick_rank(f, B - 1)
                dve.tensor_tensor(above[:], rank[:, NT, :].unsqueeze(2).broadcast_to([P, E, NT]),
                                  thresh[:], ALU.is_gt).then_inc(rank_read, 1)
                dve.wait_ge(rank_read, (f + 1) * (B + 1))
                rank_step = step(sum_rank(B - 1))
                tile_step = step(dve.tensor_reduce(ntile[:], above[:], AX_X, ALU.add))
                dve.wait_ge(dve_step, rank_step)
                rank_step = step(rank_to_int(B - 1))
                dve.wait_ge(dve_step, tile_step)
                tile_step = step(dve.tensor_tensor_scan(incl[:], ntile[:], zeros_e[:], 0.0, ALU.add, ALU.add))
                dve.wait_ge(dve_step, rank_step)
                rank_row(B - 1).then_inc(row_made, 1)
                dve.wait_ge(dve_step, tile_step)
                tile_step = step(dve.tensor_tensor(excl[:], incl[:], ntile[:], ALU.subtract))
                rank_step = step(rank_tile(B - 1))
                dve.wait_ge(dve_step, tile_step)
                link(dve.tensor_tensor(picked[:], onehot[:], excl[:].unsqueeze(1).unsqueeze(1)
                                       .broadcast_to([P, NT, TOP_K, E]), ALU.mult))
                link(dve.tensor_reduce(start_t[:], picked[:].rearrange("p t k e -> p (t k) e"), AX_X, ALU.add))
                link(dve.tensor_tensor(slot_t[:], start_t[:], rank_t[:], ALU.add))
                link(dve.tensor_tensor(in_tile[:], iota_t[:].unsqueeze(1).broadcast_to([P, J, NS]),
                                       slot_t[:].unsqueeze(2).broadcast_to([P, J, NS]), ALU.is_equal))
                for h in range(2):
                    js = slice(J // 2 * h, J // 2 * (h + 1))
                    dve.tensor_tensor(mark[:, :, js, :],
                                      in_tile[:, js, :].unsqueeze(1).broadcast_to([P, 2, J // 2, NS]),
                                      place_id[:, :, js].unsqueeze(3).broadcast_to([P, 2, J // 2, NS]),
                                      ALU.mult).then_inc(mark_made, 1)
                    if h == 0:
                        row_hots(f, B - 1)
                link(dve.tensor_tensor(passed[:], iota_t[0:1, :].unsqueeze(2).broadcast_to([1, NS, E]),
                                       incl[0:1, :].unsqueeze(1).broadcast_to([1, NS, E]), ALU.is_ge))
                link(dve.tensor_reduce(eid_f[:], passed[:], AX_X, ALU.add))
                dve.tensor_scalar(eid[:], eid_f[:], float(E - 1), None, ALU.min).then_inc(eid_made, 1)
                dve.wait_ge(list_done, f + 1)
                link(dve.tensor_scalar(place_lo[:], list_ps[:, 0, :], float(NO_PAIR), None, ALU.add))
                link(dve.tensor_tensor(place[:], list_ps[:, 1, :], place_lo[:], ALU.add))
                dve.tensor_single_scalar(tok[:], place[:], T - 1, ALU.bitwise_and).then_inc(tok_made, 1)
                for n in halves_left:
                    split_lo(dve, n, lo_made_dve)

            def experts(f):
                n0 = use_no[(f"exp{f}", 0)]

                def lo_rows(t, copied):
                    dve.wait_ge(tp_copied, copied)
                    dve.tensor_tensor(xt_lo[:, t % 2, :], tp_ps[(n0 + t) % 2][:],
                                      xt_hi[:, t % 2, :].bitcast(F32), ALU.subtract).then_inc(xt_made, 1)

                def bias(t, tile_no, done, used):
                    e = dve.value_load(eid[0:1, bass.ds(tile_no, 1)], min_val=0, max_val=E - 1)
                    dve.wait_ge(exp_done, done)
                    if used is not None:
                        dve.wait_ge(yrow_made, used)
                    dve.tensor_tensor(ypre[:, t % 2, :], y_ps[t % 2][:],
                                      be_bc[:, bass.ds(e * H, H)], ALU.add).then_inc(ypre_made, 1)

                def tile(t):
                    if t + 1 < NS:
                        lo_rows(t + 1, n0 + t + 2)
                    bias(t, t, f * NS + t + 1, f * NS + t - 1 if f or t >= 2 else None)

                dve.wait_ge(eid_made, f + 1)
                lo_rows(0, n0 + 1)
                for t in range(HEAD):
                    tile(t)
                with dve.Fori(0, LOOPS) as r:
                    for j in range(STEP):
                        t = HEAD + j
                        lo_rows(t + 1, r * STEP + (n0 + t + 2))
                        bias(t, r * STEP + t, r * STEP + (f * NS + t + 1), r * STEP + (f * NS + t - 1))
                for t in range(REST, NS):
                    tile(t)

            def add_z(f, i):
                if f == 0:
                    dve.wait_ge(z_summed, i + 1)
                    z = ZR[0][:, i % ZB, 0, :]
                    dve.tensor_tensor(x[:, i, :], x[:, i, :], z, ALU.add).then_inc(x_ffn, 1)
                else:
                    dve.wait_ge(z_in[1][i % ZT], 16 * (i // ZT + 1))
                    link(dve.tensor_tensor(x[:, i, :], x[:, i, :], ZR[1][:, i % ZT, 0, :], ALU.add))
                    dve.tensor_tensor(x[:, i, :], x[:, i, :], ZR[1][:, i % ZT, 1, :], ALU.add
                                      ).then_inc(x_ffn, 1)

            def add_z_batch(b):
                for i in range(TB * b, TB * (b + 1)):
                    add_z(0, i)
                dve.wait_ge(x_ffn, TB * (b + 1))

            def add_bv(b):
                dve.wait_ge(v_done, b + 1)
                if b >= 2:
                    dve.wait_ge(ot_done, b - 1)
                dve.tensor_tensor(v_ring[b % 2][:], v_ps[:, 0:TB * D].rearrange("p (t d) -> p t d", t=TB),
                                  bv_bc[:].unsqueeze(1).broadcast_to([P, TB, D]), ALU.add
                                  ).then_inc(v_made, 1)

            biases = [e for e in range(E) if e not in BE_ACT]
            for b in range(B):
                dve.wait_ge(x_in_sem[b], 16)
                moments("g0", b)
                if b:
                    normalise("g0", b - 1)
            normalise("g0", B - 1)
            for _ in range(2):
                copy_be(biases.pop(0))
            dve.wait_ge(const_made, CONSTS)
            todo = list(DVE_HALVES)
            for b in range(B):
                copy_be(biases.pop(0))
                if b:
                    split_rank(0, b - 1)
                choose(0, b)
                if b + 1 < B:
                    split_lo(dve, todo.pop(0), lo_made_dve)
                if b:
                    row_hots(0, b - 1)
            route(0, todo)
            experts(0)
            for b in range(2):
                add_z_batch(b)
                moments("att", b)
                normalise("att", b)
            dve.wait_ge(att_in, 16 * ATT_LOADS)
            add_bv(0)
            for b in range(B):
                dve.wait_ge(score_done, b + 1)
                if b:
                    dve.wait_ge(prob_made, TB * b)
                link(dve.tensor_reduce(smax[:], sp_ps[:].rearrange("p (q k) -> p q k", q=TB), AX_X, ALU.max))
                dve.tensor_scalar(nmax[:], smax[:], -SCALE, None, ALU.mult).then_inc(nmax_made, 1)
                if b:
                    normalise("g1", b - 1)
                if b + 2 < B:
                    add_z_batch(b + 2)
                    moments("att", b + 2)
                if b + 1 < B:
                    add_bv(b + 1)
                if b + 2 < B:
                    normalise("att", b + 2)
                if b >= 2:
                    choose(1, b - 2)
                if b >= 3:
                    split_rank(1, b - 3)
                    row_hots(1, b - 3)
                dve.wait_ge(prob_made, TB * (b + 1))
                link(dve.reciprocal(pinv[:], psumrow[:]))
                for q in range(TB):
                    i = TB * b + q
                    dve.wait_ge(bo_added, i + 1)
                    dve.wait_ge(wo_done, i + 1)
                    dve.scalar_tensor_tensor(out=x[:, i, :], in0=y_ps[q][:], scalar=pinv[:, q:q + 1],
                                             in1=x[:, i, :], op0=ALU.mult, op1=ALU.add).then_inc(x_att, 1)
                dve.wait_ge(x_att, TB * (b + 1))
                moments("g1", b)
            normalise("g1", B - 1)
            choose(1, B - 2)
            split_rank(1, B - 3)
            row_hots(1, B - 3)
            split_rank(1, B - 2)
            choose(1, B - 1)
            row_hots(1, B - 2)
            route(1, [])
            experts(1)
            for i in range(NT):
                add_z(1, i)


_INS = ['L0_attn_x', 'L0_attn_Wqkv', 'L0_attn_bqkv', 'L0_attn_Wo', 'L0_attn_bo',
        'L0_ffn_W_gate', 'L0_ffn_b_gate', 'L0_ffn_W_e', 'L0_ffn_b_e']


def kernel(**inputs):
    import numpy as _np
    import concourse.bacc as _bacc
    from concourse import mybir as _mybir
    from concourse.bass_utils import run_bass_kernel_spmd as _run

    nc = _bacc.Bacc("TRN2", target_bir_lowering=False, num_devices=1)
    arrays, args = {}, []
    for name in _INS:
        a = _np.ascontiguousarray(inputs[name])
        arrays[f"in_{name}_dram"] = a
        args.append(nc.dram_tensor(f"in_{name}_dram", a.shape, _mybir.dt.from_np(a.dtype),
                                   kind="ExternalInput").ap())
    out = nc.dram_tensor("out_0_dram", inputs['L0_attn_x'].shape, _mybir.dt.float32,
                         kind="ExternalOutput").ap()
    macaron_kernel(nc, *args, out)
    r = _run(nc, [arrays], core_ids=[0])
    return r.results[0]["out_0_dram"]
```

```python
from contextlib import ExitStack

import concourse.bass as bass
from concourse import mybir

P = 128
ALU = mybir.AluOpType
ACT = mybir.ActivationFunctionType
F32 = mybir.dt.float32
F32R = mybir.dt.float32r
BF16 = mybir.dt.bfloat16
I32 = mybir.dt.int32
U32 = mybir.dt.uint32
AX_X = mybir.AxisListType.X
EPS = 1e-5
TOP_K = 2


def macaron_kernel(nc, x_in, w_qkv, b_qkv, w_o, b_o, w_gate, b_gate, w_e, b_e, out):
    B, S, H = x_in.shape
    E, _, HO = w_e.shape
    D = w_o.shape[0]
    T = B * S
    NT = T // P
    NC = H // P
    TB = S // P
    J = NT * TOP_K
    JB = TB * TOP_K
    NS = T * TOP_K // P + E - 1
    WE = NC * H
    SCALE = float(D) ** -0.5
    HALF_MEAN = 0.5 / TOP_K
    NO_PAIR = 2 * TOP_K * T
    assert S == 2 * P and D == P and HO == H and H == 512 and NT <= 8 and NT % 2 == 0
    assert T & (T - 1) == 0

    x_rows = x_in.rearrange("b s h -> (b s) h")
    out_rows = out.rearrange("b s h -> (b s) h")

    with ExitStack() as ctx:
        def sb(name, shape, dt=F32, at=ctx):
            return at.enter_context(nc.sbuf_tensor(name, shape, dt))

        def psum(name, shape):
            return ctx.enter_context(nc.psum_tensor(name, shape, F32))

        def sem(name):
            return ctx.enter_context(nc.semaphore(name))

        xn_dram = [nc.dram_tensor(f"xn_dram{f}", [T, H], F32, kind="Internal") for f in range(2)]
        z_dram = [nc.dram_tensor(f"z_dram{f}", [TOP_K * T, H], F32, kind="Internal") for f in range(2)]

        XN = 4
        XG = 3
        YB = 3
        ZB = 2
        MR = 8
        x = sb("x", [P, NT, H])
        whi = sb("whi", [P, E * WE], F32R)
        with ExitStack() as loading:
            raw = sb("raw", [P, E * WE], at=loading)
        wlo = sb("wlo", [P, E * WE], F32R)
        be_bc = sb("be_bc", [P, E * H])
        with ExitStack() as end:
            z_mid = sb("z_mid", [P, 2, TOP_K, H], at=end)
        wqkv = sb("wqkv", [P, NC, 3 * D])
        wo = sb("wo", [P, H])
        bo_bc = sb("bo_bc", [P, H])
        wg = sb("wg", [P, NC, E])
        bg = sb("bg", [E, 1])
        bv_bc = sb("bv_bc", [P, D])
        bqk = sb("bqk", [P, 2])
        stats = sb("stats", [P, MR, 6])
        mv = sb("mv", [P, MR, 2])
        var_eps = sb("var_eps", [P, MR])
        rstd = sb("rstd", [P, MR])
        neg_half = sb("neg_half", [P, TB])
        logit_t = sb("logit_t", [E, S])
        top = sb("top", [P, TB, 8])
        topi = sb("topi", [P, TB, 8], U32)
        onehot = sb("onehot", [P, NT, TOP_K, E], BF16)
        ident = sb("ident", [P, P])
        before = sb("before", [P, P], BF16)
        ones = sb("ones", [P, P], BF16)
        iota_e = sb("iota_e", [P, E])
        iota_r = sb("iota_r", [P, P], BF16)
        iota_t = sb("iota_t", [P, NS])
        thresh = sb("thresh", [P, E, NT])
        part_id = sb("part_id", [P, 1])
        place_id = sb("place_id", [P, J])
        zeros_e = sb("zeros_e", [P, E])
        ntile = sb("ntile", [P, E])
        incl = sb("incl", [P, E])
        excl = sb("excl", [P, E])
        rank_f = sb("rank_f", [P, J])
        rank_u = sb("rank_u", [P, J], U32)
        slot_r = sb("slot_r", [P, J], U32)
        rank_t = sb("rank_t", [P, J], U32)
        start_t = sb("start_t", [P, J])
        slot_t = sb("slot_t", [P, J])
        place_lo = sb("place_lo", [P, NS])
        place = sb("place", [P, NS], U32)
        tok = sb("tok", [P, NS], U32)
        eid_f = sb("eid_f", [1, NS])
        eid = sb("eid", [1, NS], I32)
        slot_tiles = sb("slot_tiles", [1, YB, -(-NS // YB)])
        used = sb("used", [1, YB, -(-NS // YB)])
        sent_all = sb("sent_all", [1, YB])
        sent_f = sb("sent_f", [1, YB])
        sent = sb("sent", [1, YB], I32)
        nmax = sb("nmax", [P, TB])
        smax = sb("smax", [P, TB])
        psumrow = sb("psumrow", [P, TB])
        pinv = sb("pinv", [P, TB])

        with ExitStack() as shared:
            xn = sb("xn", [P, XN, H], at=shared)
            xt_gate = sb("xt_gate", [P, NC, S], at=shared)
            with ExitStack() as part:
                xn_more = sb("xn_more", [P, NT - XN, H], at=part)
                ones_row = sb("ones_row", [1, P], at=part)
                in_tile = sb("in_tile", [P, J, NS], at=part)
                mark = sb("mark", [P, 2, J, NS], BF16, at=part)
                above = sb("above", [P, E, NT], at=part)
                passed = sb("passed", [1, NS, E], at=part)
                row_hot = sb("row_hot", [P, J, P], BF16, at=part)
                picked = sb("picked", [P, NT, TOP_K, E], at=part)
            with ExitStack() as part:
                xt_att = sb("xt_att", [P, NC, S], at=part)
                qk = sb("qk", [P, 2, S], at=part)
                v_ring = [sb(f"v{i}", [P, TB, D], at=part) for i in range(2)]
                prob = sb("prob", [P, TB, S], at=part)
                pt = sb("pt", [P, TB, S], at=part)
                ot = prob[:, 0, :]
                z_rows = sb("z_rows", [P, ZB, TOP_K, H], at=part)
        with ExitStack() as shared:
            xg = sb("xg", [P, XG, H], at=shared)
            xt_hi = sb("xt_hi", [P, 2, H], F32R, at=shared)
            xt_lo = sb("xt_lo", [P, 2, H], F32R, at=shared)
            ypre = sb("ypre", [P, 2, H], at=shared)
            yrow = sb("yrow", [P, YB, H], at=shared)
        with ExitStack() as shared:
            z_last = sb("z_last", [P, NT - 2 - ZB, TOP_K, H], at=shared)

        def z_slot(f, i):
            if f == 0 or i < ZB:
                return z_rows[:, i % ZB, :, :]
            return z_mid[:, i - ZB, :, :] if i < ZB + 2 else z_last[:, i - ZB - 2, :, :]

        tp_ps = [psum(f"tp_ps{i}", [P, 512]) for i in range(2)]
        y0_ps = psum("y0_ps", [P, 512])
        qk_ps = psum("qk_ps", [P, 512])
        v_ps = psum("v_ps", [P, 512])
        sp_ps = psum("sp_ps", [P, 512])
        g_ps = psum("g_ps", [P, 512])
        rk_ps = psum("rk_ps", [P, 512])
        y_ps = [y0_ps, qk_ps]
        be_ps = [y0_ps, qk_ps, v_ps, sp_ps]
        gate_ps = g_ps[0:E, 0:S]
        logit_ps = g_ps[:, S:S + TB * E].rearrange("p (t e) -> p t e", e=E)
        rank = rk_ps[:, 0:(NT + 1) * E].rearrange("p (t e) -> p t e", e=E)
        list_ps = g_ps[:, 0:2 * NS].rearrange("p (a t) -> p a t", a=2)

        PE_CONSTS = 3
        CONSTS = 12 + YB
        ATT_LOADS = 5
        x_in_sem = [sem(f"x_loaded{b}") for b in range(B)]
        gate_in = sem("gate_weights_loaded")
        be_in = sem("be_loaded")
        raw_in = [sem(f"raw_loaded{n}") for n in range(2 * E)]
        att_in = sem("attention_weights_loaded")
        const_made = sem("const_made")
        const_step = sem("const_step")
        be_done = sem("be_done")
        be_copied = sem("be_copied")
        be_copied_act = sem("be_copied_act")
        hi_made = sem("hi_made")
        lo_made_dve = sem("lo_made_dve")
        lo_made_pool = sem("lo_made_pool")
        dve_step = sem("dve_step")
        var_made = sem("var_made")
        rstd_made = sem("rstd_made")
        xn_made = sem("xn_made")
        xn_stored = [sem(f"xn_stored{s}") for s in range(NT)]
        tp_full = sem("tp_full")
        tp_copied = sem("tp_copied")
        gate_done = sem("gate_done")
        gate_copied = sem("gate_copied")
        logit_done = sem("logit_done")
        logit_read = sem("logit_read")
        onehot_made = sem("onehot_made")
        rank_done = sem("rank_done")
        rank_read = sem("rank_read")
        in_tile_made = sem("in_tile_made")
        mark_made = sem("mark_made")
        row_made = sem("row_made")
        row_hot_made = sem("row_hot_made")
        list_done = sem("list_done")
        tok_made = sem("tok_made")
        eid_made = sem("eid_made")
        sent_made = sem("sent_made")
        gathered = [sem(f"gathered{s}") for s in range(XG)]
        xt_made = sem("xt_made")
        exp_done = sem("exp_done")
        ypre_made = sem("ypre_made")
        yrow_made = sem("yrow_made")
        scattered = [sem(f"scattered{s}") for s in range(YB)]
        z_in = [[sem(f"z_loaded{f}_{s}") for s in range((ZB, NT)[f])] for f in range(2)]
        z_first = [[sem(f"z_first{i}_{k}") for k in range(TOP_K)] for i in range(TB)]
        z_summed = sem("z_summed")
        x_ffn = sem("x_ffn")
        bo_added = sem("bo_added")
        qk_done = sem("qk_done")
        qk_copied = sem("qk_copied")
        v_done = sem("v_done")
        v_made = sem("v_made")
        score_done = sem("score_done")
        nmax_made = sem("nmax_made")
        prob_made = sem("prob_made")
        pt_done = sem("pt_done")
        pt_copied = sem("pt_copied")
        ot_done = sem("ot_done")
        ot_copied = sem("ot_copied")
        wo_done = sem("wo_done")
        x_att = sem("x_att")
        out_stored = sem("out_stored")

        def of(kind, b):
            return [(kind, i) for i in range(TB * b, TB * (b + 1))]

        tp_uses = [u for b in range(B) for u in of("g0", b)] + [("exp0", t) for t in range(NS)]
        tp_uses += of("att", 0)
        norms = [u for b in range(B) for u in of("g0", b)] + of("att", 0) + of("att", 1)
        for b in range(B):
            tp_uses += (of("att", b + 1) if b + 1 < B else []) + (of("g1", b - 1) if b else [])
            norms += (of("g1", b - 1) if b else []) + (of("att", b + 2) if b + 2 < B else [])
        norms += of("g1", B - 1)
        tp_uses += of("g1", B - 1) + [("exp1", t) for t in range(NS)]
        use_no = {u: n for n, u in enumerate(tp_uses)}
        norm_no = {u: n for n, u in enumerate(norms)}

        def xn_slot(n):
            return n if n < NT else n % XN

        def xn_at(n):
            s = xn_slot(n)
            return xn[:, s, :] if s < XN else xn_more[:, s - XN, :]

        def last_in_slot(n):
            return next((m for m in range(n - 1, -1, -1) if xn_slot(m) == xn_slot(n)), None)

        def stores_from(s, upto):
            return sum(1 for n in range(upto) if xn_slot(n) == s and norms[n][0] != "att")

        SUM_END = [3, 5, 7]
        MARK_AT = 13
        WARM = [14, 10]
        WARM_SPLIT = 6
        WARM_ATT = 14
        AHEAD = 5

        DVE_HALVES = [1, 3, 5, 7, 12, 13, 14, 15]
        POOL_HALVES = [n for n in range(2 * E) if n not in DVE_HALVES]

        BE_ACT = [E - 2, E - 1]

        def half(w, n):
            return w[:, n * (WE // 2):(n + 1) * (WE // 2)]

        def split_lo(eng, n, done):
            eng.wait_ge(hi_made, n + 1)
            eng.tensor_tensor(half(wlo, n), half(raw, n), half(whi, n).bitcast(F32),
                              ALU.subtract).then_inc(done, 1)

        HEAD, STEP = 2, 6
        LOOPS = (NS - 1 - HEAD) // STEP
        REST = HEAD + LOOPS * STEP

        def slot_uses(ring, s):
            return sum(1 for t in range(NS) if t % ring == s)

        block = ctx.enter_context(nc.Block())

        @block.sync
        def _(sp):
            for b in range(B):
                sp.dma_start(x[:, TB * b:TB * (b + 1), :],
                             x_rows[b * S:(b + 1) * S, :].rearrange("(t p) h -> p t h", p=P)
                             ).then_inc(x_in_sem[b], 16)
            for n in range(2 * E):
                if n >= AHEAD:
                    sp.wait_ge(hi_made, n - AHEAD + 1)
                rows = w_e[n // 2].rearrange("(c p) h -> p c h", p=P)
                sp.dma_start(half(raw, n).rearrange("p (c h) -> p c h", h=H),
                             rows[:, NC // 2 * (n % 2):NC // 2 * (n % 2 + 1), :]
                             ).then_inc(raw_in[n], 16)
            sp.wait_ge(gathered[XG - 1], 16)
            sp.dma_start(wqkv[:], w_qkv.rearrange("(c p) n -> p c n", p=P)).then_inc(att_in, 16)
            sp.dma_start(wo[:], w_o).then_inc(att_in, 16)
            sp.dma_start(bqk[:], b_qkv[0:2 * D].rearrange("(j d) -> d j", j=2),
                         allow_slow_non_contiguous=True).then_inc(att_in, 16)
            sp.dma_start(bv_bc[:], b_qkv[2 * D:3 * D].partition_broadcast(P)).then_inc(att_in, 16)
            sp.dma_start(bo_bc[:], b_o.partition_broadcast(P)).then_inc(att_in, 16)

            def wait_scatters(f):
                sp.wait_ge(sent_made, f + 1)
                counts = [sp.value_load(sent[0:1, s:s + 1], min_val=16 * (T * TOP_K // P // YB),
                                        max_val=16 * 2 * NS) for s in range(YB)]
                for s in range(YB):
                    sp.wait_ge(scattered[s], counts[s])

            def load_z(f, i):
                ring = (ZB, NT)[f]
                if f == 0 and i >= ZB:
                    sp.wait_ge(x_ffn, i - ZB + 1)
                if f and i == ZB + 2:
                    sp.wait_ge(tp_full, len(tp_uses))
                if f and i == ZB + 3:
                    sp.wait_ge(exp_done, 2 * NS)
                    sp.wait_ge(yrow_made, 2 * NS)
                if f == 0 and i < TB:
                    for k in range(TOP_K):
                        sp.dma_start(z_slot(f, i)[:, k, :],
                                     z_dram[f].rearrange("(k t p) h -> k t p h", k=TOP_K, p=P)[k, i]
                                     ).then_inc(z_first[i][k], 16)
                    return
                sp.dma_start(z_slot(f, i),
                             z_dram[f].rearrange("(k t p) h -> t p k h", k=TOP_K, p=P)[i]
                             ).then_inc(z_in[f][i % ring], 16)

            for f in range(2):
                wait_scatters(f)
                for i in range(NT):
                    load_z(f, i)
            for i in range(NT):
                sp.wait_ge(x_ffn, NT + i + 1)
                sp.dma_start(out_rows[i * P:(i + 1) * P, :], x[:, i, :]).then_inc(out_stored, 16)
            for s in range(YB):
                sp.wait_ge(scattered[s], 16 * 2 * slot_uses(YB, s))
            sp.wait_ge(out_stored, 16 * NT)

        @block.gpsimd
        def _(pool):
            steps = [0]

            def link(ins):
                steps[0] += 1
                ins.then_inc(const_step, 1)
                pool.wait_ge(const_step, steps[0])

            pool.memset(ones_row[:], 1.0).then_inc(const_made, 1)
            link(pool.memset(ident[:], 0.0))
            pool.affine_select(out=ident[:], in_=ident[:], compare_op=ALU.not_equal, fill=1.0, base=0,
                               pattern=[[-1, P]], channel_multiplier=1).then_inc(const_made, 1)
            link(pool.memset(ones[:], 1.0))
            pool.affine_select(out=before[:], in_=ones[:], compare_op=ALU.is_gt, fill=0.0, base=0,
                               pattern=[[1, P]], channel_multiplier=-1).then_inc(const_made, 1)
            pool.memset(neg_half[:], -0.5).then_inc(const_made, 1)
            pool.iota(iota_e[:], pattern=[[1, E]], base=0, channel_multiplier=0,
                      allow_small_or_imprecise_dtypes=True).then_inc(const_made, 1)
            pool.iota(iota_r[:], pattern=[[1, P]], base=0, channel_multiplier=0,
                      allow_small_or_imprecise_dtypes=True).then_inc(const_made, 1)
            pool.iota(iota_t[:], pattern=[[1, NS]], base=0, channel_multiplier=0,
                      allow_small_or_imprecise_dtypes=True).then_inc(const_made, 1)
            pool.iota(thresh[:], pattern=[[0, E], [P, NT]], base=0, channel_multiplier=0,
                      allow_small_or_imprecise_dtypes=True).then_inc(const_made, 1)
            pool.iota(part_id[:], pattern=[[0, 1]], base=0, channel_multiplier=1,
                      allow_small_or_imprecise_dtypes=True).then_inc(const_made, 1)
            pool.iota(place_id[:].rearrange("p (t k) -> p t k", k=TOP_K), pattern=[[P, NT], [T, TOP_K]],
                      base=-NO_PAIR, channel_multiplier=0,
                      allow_small_or_imprecise_dtypes=True).then_inc(const_made, 1)
            pool.memset(zeros_e[:], 0.0).then_inc(const_made, 1)
            for s in range(YB):
                pool.memset(sent_all[:, s:s + 1], 16.0 * slot_uses(YB, s)).then_inc(const_made, 1)
            pool.iota(slot_tiles[:], pattern=[[1, YB], [YB, -(-NS // YB)]], base=0, channel_multiplier=0,
                      allow_small_or_imprecise_dtypes=True).then_inc(const_made, 1)

            pool.wait_ge(const_made, CONSTS)

            def deviations(kind, b):
                n = norm_no[(kind, TB * b)]
                s = n % MR
                pool.wait_ge(var_made, n // TB + 1)
                if n >= MR:
                    pool.wait_ge(xn_made, n - MR + TB)
                pool.tensor_tensor(rstd[:, s:s + TB], var_eps[:, s:s + TB], neg_half[:], ALU.pow
                                   ).then_inc(rstd_made, 1)

            def gather(f, t):
                if t >= XG:
                    pool.wait_ge(tp_full, use_no[(f"exp{f}", t - XG)] + 1)
                pool.indirect_dma_start(
                    out=xg[:, t % XG, :], out_offset=None, in_=xn_dram[f][:, :],
                    in_offset=bass.IndirectOffsetOnAxis(ap=tok[:, t:t + 1], axis=0)
                ).then_inc(gathered[t % XG], 16)

            def scatter(f, t):
                pool.wait_ge(yrow_made, f * NS + t + 1)
                pool.indirect_dma_start(
                    out=z_dram[f][:, :], out_offset=bass.IndirectOffsetOnAxis(ap=place[:, t:t + 1], axis=0),
                    in_=yrow[:, t % YB, :], in_offset=None, bounds_check=TOP_K * T - 1, oob_is_err=False
                ).then_inc(scattered[t % YB], 16)

            def experts(f):
                pool.wait_ge(tok_made, f + 1)
                for s in range(NT):
                    pool.wait_ge(xn_stored[s], 16 * stores_from(s, len(norms) if f else NT))
                for t in range(XG + 1):
                    gather(f, t)
                for t in range(NS):
                    if t + XG + 1 < NS:
                        gather(f, t + XG + 1)
                    scatter(f, t)

            def sum_z(f, i):
                if f:
                    pool.wait_ge(z_in[1][i], 16)
                else:
                    pool.wait_ge(z_in[0][i % ZB], 16 * (i // ZB))
                z = z_slot(f, i)
                pool.tensor_tensor(z[:, 0, :], z[:, 0, :], z[:, 1, :], ALU.add).then_inc(z_summed, 1)

            def add_bo(b):
                for i in range(TB * b, TB * (b + 1)):
                    pool.wait_ge(xn_made, norm_no[("att", i)] + 1)
                    pool.tensor_tensor(x[:, i, :], x[:, i, :], bo_bc[:], ALU.add).then_inc(bo_added, 1)

            def attention_input(b):
                for i in range(TB * b, TB * (b + 1)):
                    sum_z(0, i)
                deviations("att", b)

            for b in range(B):
                deviations("g0", b)
            for n in POOL_HALVES:
                split_lo(pool, n, lo_made_pool)
            experts(0)
            pool.wait_ge(att_in, 16 * ATT_LOADS)
            deviations("att", 0)
            attention_input(1)
            add_bo(0)
            add_bo(1)
            for b in range(B):
                if b + 2 < B:
                    for i in range(TB * (b + 2), TB * (b + 3)):
                        sum_z(0, i)
                if b:
                    deviations("g1", b - 1)
                if b + 2 < B:
                    deviations("att", b + 2)
                    add_bo(b + 2)
            deviations("g1", B - 1)
            experts(1)
            for i in SUM_END:
                sum_z(1, i)

        @block.scalar
        def _(act):
            act.dma_start(be_bc[0:1, :], b_e.rearrange("(a e) h -> a (e h)", a=1)).then_inc(be_in, 16)
            act.dma_start(wg[:], w_gate.rearrange("(c p) e -> p c e", p=P)).then_inc(gate_in, 16)
            act.dma_start(bg[:], b_gate.rearrange("(e a) -> e a", a=1),
                          allow_slow_non_contiguous=True).then_inc(gate_in, 16)

            def split_hi(n):
                act.wait_ge(raw_in[n], 16)
                act.activation(half(whi, n), half(raw, n), ACT.Copy).then_inc(hi_made, 1)

            def store_xn(f, i):
                m = norm_no[(f"g{f}", i)]
                act.wait_ge(xn_made, m + 1)
                act.dma_start(xn_dram[f][i * P:(i + 1) * P, :], xn_at(m)
                              ).then_inc(xn_stored[xn_slot(m)], 16)

            def copy_gate(f, b):
                for i in range(TB * b, TB * (b + 1)):
                    n = use_no[(f"g{f}", i)]
                    store_xn(f, i)
                    if f * B + b:
                        act.wait_ge(gate_done, f * B + b)
                    act.wait_ge(tp_full, n + 1)
                    act.activation(xt_gate[:, :, (i % TB) * P:(i % TB + 1) * P],
                                   tp_ps[n % 2][:].rearrange("p (c t) -> p c t", c=NC),
                                   ACT.Copy).then_inc(tp_copied, 1)

            def copy_logits(f, b):
                m = f * B + b
                act.wait_ge(gate_done, m + 1)
                if m:
                    act.wait_ge(logit_done, m)
                act.activation(logit_t[:], gate_ps, ACT.Identity, bias=bg[:]).then_inc(gate_copied, 1)

            def copy_att(b):
                for i in range(TB * b, TB * (b + 1)):
                    n = use_no[("att", i)]
                    if b:
                        act.wait_ge(v_done, b)
                    act.wait_ge(tp_full, n + 1)
                    act.activation(xt_att[:, :, (i % TB) * P:(i % TB + 1) * P],
                                   tp_ps[n % 2][:].rearrange("p (c t) -> p c t", c=NC),
                                   ACT.Copy).then_inc(tp_copied, 1)

            def mark_partition(f):
                act.wait_ge(in_tile_made, f + 1)
                act.activation(mark[:, 0, :, :], in_tile[:], ACT.Identity, scale=part_id[:]
                               ).then_inc(mark_made, 1)

            def experts(f):
                n0 = use_no[(f"exp{f}", 0)]

                def hi_rows(t, full, done):
                    act.wait_ge(tp_full, full)
                    if done is not None:
                        act.wait_ge(exp_done, done)
                    act.activation(xt_hi[:, t % 2, :], tp_ps[(n0 + t) % 2][:], ACT.Copy
                                   ).then_inc(tp_copied, 1)

                def relu(t, made, sent):
                    act.wait_ge(ypre_made, made)
                    if sent is not None:
                        act.wait_ge(scattered[t % YB], sent)
                    act.activation(yrow[:, t % YB, :], ypre[:, t % 2, :], ACT.Relu,
                                   scale=HALF_MEAN).then_inc(yrow_made, 1)

                def sent(t):
                    return 16 * (f * slot_uses(YB, t % YB) + t // YB)

                def tile(t):
                    if t + 1 < NS:
                        hi_rows(t + 1, n0 + t + 2, f * NS + t or None)
                    relu(t, f * NS + t + 1, sent(t) or None)

                hi_rows(0, n0 + 1, None)
                for t in range(HEAD + STEP):
                    tile(t)
                with act.Fori(1, LOOPS) as r:
                    for j in range(STEP):
                        t = HEAD + j
                        hi_rows(t + 1, r * STEP + (n0 + t + 2), r * STEP + (f * NS + t))
                        relu(t, r * STEP + (f * NS + t + 1), r * (16 * STEP // YB) + sent(t))
                for t in range(REST, NS):
                    tile(t)

            def copy_qk(b):
                act.wait_ge(qk_done, b + 1)
                if b:
                    act.wait_ge(score_done, b)
                for j in range(2):
                    act.activation(qk[:, j, :], qk_ps[:, j * S:(j + 1) * S], ACT.Identity,
                                   bias=bqk[:, j:j + 1]).then_inc(qk_copied, 1)

            def softmax(b):
                act.wait_ge(nmax_made, b + 1)
                if b:
                    act.wait_ge(wo_done, TB * b)
                    act.wait_ge(x_att, TB * b)
                for q in range(TB):
                    act.activation(prob[:, q, :], sp_ps[:, q * S:(q + 1) * S], ACT.Exp,
                                   bias=nmax[:, q:q + 1], scale=SCALE,
                                   accum_out=psumrow[:, q:q + 1]).then_inc(prob_made, 1)

            act.wait_ge(gate_in, 32)
            for b in range(B):
                if b:
                    copy_logits(0, b - 1)
                copy_gate(0, b)
                for n in range(2 * b + 2 if b else 0, 2 * b + 4):
                    split_hi(n)
            copy_logits(0, B - 1)
            for n in range(2 * B + 2, MARK_AT):
                split_hi(n)
            mark_partition(0)
            for n in range(MARK_AT, 2 * E):
                split_hi(n)
            for e in BE_ACT:
                act.wait_ge(be_done, e + 1)
                act.activation(be_bc[:, e * H:(e + 1) * H], be_ps[e % len(be_ps)][:], ACT.Copy
                               ).then_inc(be_copied_act, 1)
            experts(0)
            act.wait_ge(att_in, 16 * ATT_LOADS)
            copy_att(0)
            copy_qk(0)
            for b in range(B):
                if b + 1 < B:
                    copy_att(b + 1)
                if b == 0:
                    for s in range(YB):
                        act.wait_ge(scattered[s], 16 * slot_uses(YB, s))
                softmax(b)
                if b >= 2:
                    copy_logits(1, b - 2)
                if b + 1 < B:
                    copy_qk(b + 1)
                act.wait_ge(pt_done, b + 1)
                if b:
                    act.wait_ge(ot_done, b)
                act.activation(pt[:].rearrange("p t s -> p (t s)"), sp_ps[:], ACT.Copy
                               ).then_inc(pt_copied, 1)
                act.wait_ge(ot_done, b + 1)
                act.activation(ot, sp_ps[:, 0:S], ACT.Copy).then_inc(ot_copied, 1)
                if b:
                    copy_gate(1, b - 1)
            copy_logits(1, B - 2)
            copy_gate(1, B - 1)
            copy_logits(1, B - 1)
            mark_partition(1)
            experts(1)

        @block.tensor
        def _(pe):
            def warm_up(n, bank=rk_ps):
                for _ in range(n):
                    pe.matmul(bank[:], ones[:], ones[:].unsqueeze(1).broadcast_to([P, 4, P]),
                              start=True, stop=True)

            def broadcast_be(e):
                if e >= len(be_ps):
                    pe.wait_ge(be_copied, e - len(be_ps) + 1)
                pe.matmul(be_ps[e % len(be_ps)][:], ones_row[:], be_bc[0:1, e * H:(e + 1) * H],
                          start=True, stop=True).then_inc(be_done, 1)

            def transpose_xn(kind, b):
                for i in range(TB * b, TB * (b + 1)):
                    n, m = use_no[(kind, i)], norm_no[(kind, i)]
                    pe.wait_ge(xn_made, m + 1)
                    if n >= 2:
                        if n - 2 in exp_uses:
                            pe.wait_ge(xt_made, exp_uses[n - 2] + 1)
                        else:
                            pe.wait_ge(tp_copied, n - 1)
                    for c in range(NC):
                        last = pe.transpose(tp_ps[n % 2][:, c * P:(c + 1) * P],
                                            xn_at(m)[:, c * P:(c + 1) * P], ident[:])
                    last.then_inc(tp_full, 1)

            exp_uses = {n: int(kind[-1]) * NS + t for n, (kind, t) in enumerate(tp_uses) if kind[:3] == "exp"}

            def gate(f, b):
                pe.wait_ge(tp_copied, use_no[(f"g{f}", TB * (b + 1) - 1)] + 1)
                if f * B + b:
                    pe.wait_ge(logit_read, f * B + b)
                for c in range(NC):
                    last = pe.matmul(gate_ps, wg[:, c, :], xt_gate[:, c, :],
                                     start=(c == 0), stop=(c == NC - 1))
                last.then_inc(gate_done, 1)

            def transpose_logits(f, b):
                pe.wait_ge(gate_copied, f * B + b + 1)
                for i in range(TB):
                    last = pe.transpose(logit_ps[:, i, :], logit_t[:, i * P:(i + 1) * P], ident[0:E, 0:E])
                last.then_inc(logit_done, 1)

            def count(f, b):
                pe.wait_ge(onehot_made, f * B + b + 1)
                if b:
                    pe.wait_ge(rank_read, f * (B + 1) + b)
                elif f:
                    pe.wait_ge(rank_read, B + 1)
                for i in range(TB * b, TB * (b + 1)):
                    for k in range(TOP_K):
                        pe.matmul(rank[:, i, :], before[:], onehot[:, i, k, :],
                                  start=(i == 0 and k == 0), stop=False, skip_group_check=True)
                        rest = onehot[:, i, k, :].unsqueeze(1).broadcast_to([P, NT - i, E])
                        last = pe.matmul(rank[:, i + 1:NT + 1, :], ones[:], rest,
                                         start=False, stop=(i == NT - 1 and k == TOP_K - 1),
                                         skip_group_check=True)
                last.then_inc(rank_done, 1)

            def token_list(f):
                pe.wait_ge(mark_made, 2 * (f + 1))
                for j in range(J):
                    if j % JB == 0:
                        pe.wait_ge(row_hot_made, (f * J + j) // JB + 1)
                    last = pe.matmul(list_ps, row_hot[:, j, :], mark[:, :, j, :],
                                     start=(j == 0), stop=(j == J - 1))
                last.then_inc(list_done, 1)
                warm_up(WARM[f])

            def experts(f):
                n0 = use_no[(f"exp{f}", 0)]

                def transposes(t, landed, free_sem, free):
                    pe.wait_ge(gathered[t % XG], landed)
                    pe.wait_ge(free_sem, free)
                    for c in range(NC):
                        last = pe.transpose(tp_ps[(n0 + t) % 2][:, c * P:(c + 1) * P],
                                            xg[:, t % XG, c * P:(c + 1) * P], ident[:])
                    last.then_inc(tp_full, 1)

                def product(t, tile_no, copied, made, read):
                    e = pe.value_load(eid[0:1, bass.ds(tile_no, 1)], min_val=0, max_val=E - 1)
                    pe.wait_ge(tp_copied, copied)
                    if read is not None:
                        pe.wait_ge(ypre_made, read)
                    n = 0
                    for rows, w in ((xt_hi, whi), (xt_hi, wlo), (xt_lo, whi)):
                        if rows is xt_lo:
                            pe.wait_ge(xt_made, made)
                        for c in range(NC):
                            last = pe.matmul(y_ps[t % 2][:], rows[:, t % 2, c * P:(c + 1) * P],
                                             w[:, bass.ds(e * WE + c * H, H)],
                                             start=(n == 0), stop=(n == 3 * NC - 1))
                            n += 1
                    last.then_inc(exp_done, 1)

                def landed(t):
                    return 16 * (f * slot_uses(XG, t % XG) + t // XG + 1)

                def tile(t):
                    if t + 1 < NS:
                        if t:
                            transposes(t + 1, landed(t + 1), xt_made, f * NS + t)
                        else:
                            transposes(t + 1, landed(t + 1), tp_copied, n0)
                    product(t, t, n0 + t + 1, f * NS + t + 1, f * NS + t - 1 if f or t >= 2 else None)

                transposes(0, landed(0), tp_copied, n0 - 1)
                pe.wait_ge(eid_made, f + 1)
                if f == 0:
                    warm_up(WARM_SPLIT)
                    pe.wait_ge(lo_made_dve, len(DVE_HALVES))
                    pe.wait_ge(lo_made_pool, len(POOL_HALVES))
                    pe.wait_ge(be_copied, E - len(BE_ACT))
                    pe.wait_ge(be_copied_act, len(BE_ACT))
                for t in range(HEAD):
                    tile(t)
                with pe.Fori(0, LOOPS) as r:
                    for j in range(STEP):
                        t = HEAD + j
                        transposes(t + 1, r * (16 * STEP // XG) + landed(t + 1), xt_made,
                                   r * STEP + (f * NS + t))
                        product(t, r * STEP + t, r * STEP + (n0 + t + 1), r * STEP + (f * NS + t + 1),
                                r * STEP + (f * NS + t - 1))
                for t in range(REST, NS):
                    tile(t)

            def project_qk(b):
                pe.wait_ge(tp_copied, use_no[("att", TB * (b + 1) - 1)] + 1)
                if b:
                    pe.wait_ge(qk_copied, 2 * b)
                else:
                    pe.wait_ge(ypre_made, NS)
                if b >= 2:
                    pe.wait_ge(x_att, TB * (b - 1))
                for j in range(2):
                    for c in range(NC):
                        last = pe.matmul(qk_ps[:, j * S:(j + 1) * S], wqkv[:, c, j * D:(j + 1) * D],
                                         xt_att[:, c, :], start=(c == 0), stop=(c == NC - 1))
                last.then_inc(qk_done, 1)

            def project_v(b):
                if b:
                    pe.wait_ge(v_made, b)
                for i in range(TB):
                    for c in range(NC):
                        last = pe.matmul(v_ps[:, i * D:(i + 1) * D], xt_att[:, c, i * P:(i + 1) * P],
                                         wqkv[:, c, 2 * D:3 * D], start=(c == 0), stop=(c == NC - 1))
                last.then_inc(v_done, 1)

            def scores(b):
                pe.wait_ge(qk_copied, 2 * (b + 1))
                if b:
                    pe.wait_ge(ot_copied, b)
                for q in range(TB):
                    last = pe.matmul(sp_ps[:, q * S:(q + 1) * S], qk[:, 0, q * P:(q + 1) * P],
                                     qk[:, 1, :], start=True, stop=True)
                last.then_inc(score_done, 1)

            def transpose_prob(b):
                pe.wait_ge(prob_made, TB * (b + 1))
                for k in range(TB):
                    for q in range(TB):
                        last = pe.transpose(sp_ps[:, k * S + q * P:k * S + (q + 1) * P],
                                            prob[:, q, k * P:(k + 1) * P], ident[:])
                last.then_inc(pt_done, 1)

            def mix_v(b):
                pe.wait_ge(pt_copied, b + 1)
                pe.wait_ge(v_made, b + 1)
                for k in range(TB):
                    last = pe.matmul(sp_ps[:, 0:S], v_ring[b % 2][:, k, :], pt[:, k, :],
                                     start=(k == 0), stop=(k == TB - 1))
                last.then_inc(ot_done, 1)

            def project_out(b):
                pe.wait_ge(ot_copied, b + 1)
                pe.wait_ge(qk_copied, 2 * min(b + 2, B))
                if b:
                    pe.wait_ge(x_att, TB * b)
                for q in range(TB):
                    pe.matmul(y_ps[q][:], ot[:, q * P:(q + 1) * P], wo[:], start=True, stop=True
                              ).then_inc(wo_done, 1)

            pe.wait_ge(const_made, PE_CONSTS)
            warm_up(6)
            pe.wait_ge(be_in, 16)
            biases = list(range(E))
            for _ in range(2):
                broadcast_be(biases.pop(0))
            for b in range(B):
                transpose_xn("g0", b)
                if b:
                    transpose_logits(0, b - 1)
                broadcast_be(biases.pop(0))
                if b == 0:
                    pe.wait_ge(gate_in, 32)
                gate(0, b)
                if b:
                    count(0, b - 1)
            broadcast_be(biases.pop(0))
            transpose_logits(0, B - 1)
            count(0, B - 1)
            broadcast_be(biases.pop(0))
            token_list(0)
            experts(0)
            pe.wait_ge(z_first[0][0], 16)
            warm_up(WARM_ATT)
            pe.wait_ge(att_in, 16 * ATT_LOADS)
            transpose_xn("att", 0)
            warm_up(2)
            project_qk(0)
            project_v(0)
            for b in range(B):
                if b + 1 < B:
                    transpose_xn("att", b + 1)
                scores(b)
                if b >= 2:
                    gate(1, b - 2)
                if b + 1 < B:
                    project_qk(b + 1)
                if b >= 2:
                    transpose_logits(1, b - 2)
                transpose_prob(b)
                if b + 1 < B:
                    project_v(b + 1)
                mix_v(b)
                if b:
                    transpose_xn("g1", b - 1)
                project_out(b)
                if b >= 2:
                    count(1, b - 2)
            gate(1, B - 2)
            transpose_logits(1, B - 2)
            warm_up(3, v_ps)
            transpose_xn("g1", B - 1)
            count(1, B - 2)
            gate(1, B - 1)
            transpose_logits(1, B - 1)
            count(1, B - 1)
            token_list(1)
            experts(1)

        @block.vector
        def _(dve):
            steps = [0]

            def step(ins):
                steps[0] += 1
                ins.then_inc(dve_step, 1)
                return steps[0]

            def link(ins):
                dve.wait_ge(dve_step, step(ins))

            def copy_be(e):
                dve.wait_ge(be_done, e + 1)
                dve.tensor_copy(be_bc[:, e * H:(e + 1) * H], be_ps[e % len(be_ps)][:]).then_inc(be_copied, 1)

            def moments(kind, b):
                n = norm_no[(kind, TB * b)]
                s = n % MR
                read = []
                for i in range(TB):
                    if (kind, b) == ("att", 0):
                        add_z(0, i)
                        dve.wait_ge(x_ffn, i + 1)
                    read.append(step(dve.bn_stats(stats[:, s + i, :], x[:, TB * b + i, :])))
                for i in range(TB):
                    dve.wait_ge(dve_step, read[i])
                    last = step(dve.bn_aggr(mv[:, s + i, :], stats[:, s + i, :]))
                dve.wait_ge(dve_step, last)
                if n >= MR:
                    dve.wait_ge(rstd_made, (n - MR) // TB + 1)
                dve.tensor_scalar(var_eps[:, s:s + TB], mv[:, s:s + TB, 1], EPS, None,
                                  ALU.add).then_inc(var_made, 1)

            def normalise(kind, b):
                for i in range(TB * b, TB * (b + 1)):
                    n = norm_no[(kind, i)]
                    s = n % MR
                    if last_in_slot(n) is not None:
                        dve.wait_ge(tp_full, use_no[norms[last_in_slot(n)]] + 1)
                        if stores_from(xn_slot(n), n):
                            dve.wait_ge(xn_stored[xn_slot(n)], 16 * stores_from(xn_slot(n), n))
                    dve.wait_ge(rstd_made, n // TB + 1)
                    dve.tensor_scalar(xn_at(n), x[:, i, :], mv[:, s, 0:1], rstd[:, s:s + 1],
                                      ALU.subtract, ALU.mult).then_inc(xn_made, 1)

            def choose(f, b):
                m = f * B + b
                dve.wait_ge(logit_done, m + 1)
                tops = [step(dve.max(top[:, i, :], logit_ps[:, i, :])) for i in range(TB)]
                for i in range(TB):
                    dve.wait_ge(dve_step, tops[i])
                    last = dve.max_index(topi[:, i, :], top[:, i, :], logit_ps[:, i, :])
                    if i + 1 < TB:
                        step(last)
                last.then_inc(logit_read, 1)
                dve.wait_ge(logit_read, m + 1)
                dve.tensor_tensor(onehot[:, TB * b:TB * (b + 1), :, :],
                                  iota_e[:].unsqueeze(1).unsqueeze(1).broadcast_to([P, TB, TOP_K, E]),
                                  topi[:, :, 0:TOP_K].unsqueeze(3).broadcast_to([P, TB, TOP_K, E]),
                                  ALU.is_equal).then_inc(onehot_made, 1)

            def pair_columns(b):
                return slice(JB * b, JB * (b + 1))

            def pick_rank(f, b):
                tiles = slice(TB * b, TB * (b + 1))
                dve.wait_ge(rank_done, f * B + b + 1)
                dve.tensor_tensor(picked[:, tiles], onehot[:, tiles],
                                  rank[:, tiles, :].unsqueeze(2).broadcast_to([P, TB, TOP_K, E]),
                                  ALU.mult).then_inc(rank_read, 1)

            def sum_rank(b):
                tiles = slice(TB * b, TB * (b + 1))
                return dve.tensor_reduce(rank_f[:, pair_columns(b)],
                                         picked[:, tiles].rearrange("p t k e -> p (t k) e"), AX_X, ALU.add)

            def rank_to_int(b):
                return dve.tensor_copy(rank_u[:, pair_columns(b)], rank_f[:, pair_columns(b)])

            def rank_row(b):
                return dve.tensor_single_scalar(slot_r[:, pair_columns(b)], rank_u[:, pair_columns(b)],
                                                P - 1, ALU.bitwise_and)

            def rank_tile(b):
                return dve.tensor_single_scalar(rank_t[:, pair_columns(b)], rank_u[:, pair_columns(b)],
                                                P.bit_length() - 1, ALU.logical_shift_right)

            def split_rank(f, b):
                pick_rank(f, b)
                dve.wait_ge(rank_read, f * (B + 1) + b + 1)
                link(sum_rank(b))
                link(rank_to_int(b))
                rank_row(b).then_inc(row_made, 1)
                step(rank_tile(b))

            def row_hots(f, b):
                dve.wait_ge(row_made, f * B + b + 1)
                dve.tensor_tensor(row_hot[:, pair_columns(b), :],
                                  iota_r[:].unsqueeze(1).broadcast_to([P, JB, P]),
                                  slot_r[:, pair_columns(b)].unsqueeze(2).broadcast_to([P, JB, P]),
                                  ALU.is_equal).then_inc(row_hot_made, 1)

            def tile_experts(f):
                link(dve.tensor_tensor(passed[:], iota_t[0:1, :].unsqueeze(2).broadcast_to([1, NS, E]),
                                       incl[0:1, :].unsqueeze(1).broadcast_to([1, NS, E]), ALU.is_ge))
                link(dve.tensor_reduce(eid_f[:], passed[:], AX_X, ALU.add))
                dve.tensor_scalar(eid[:], eid_f[:], float(E - 1), None, ALU.min).then_inc(eid_made, 1)

            def count_sent(f):
                link(dve.tensor_tensor(used[:], slot_tiles[:],
                                       incl[0:1, E - 1:E].unsqueeze(2).broadcast_to([1, YB, -(-NS // YB)]),
                                       ALU.is_lt))
                link(dve.tensor_reduce(sent_f[:], used[:], AX_X, ALU.add))
                if f == 0:
                    dve.tensor_scalar(sent[:], sent_f[:], 16.0, None, ALU.mult).then_inc(sent_made, 1)
                else:
                    link(dve.tensor_scalar(sent_f[:], sent_f[:], 16.0, None, ALU.mult))
                    dve.tensor_tensor(sent[:], sent_f[:], sent_all[:], ALU.add).then_inc(sent_made, 1)

            def route(f, halves_left):
                pick_rank(f, B - 1)
                dve.tensor_tensor(above[:], rank[:, NT, :].unsqueeze(2).broadcast_to([P, E, NT]),
                                  thresh[:], ALU.is_gt).then_inc(rank_read, 1)
                dve.wait_ge(rank_read, (f + 1) * (B + 1))
                rank_step = step(sum_rank(B - 1))
                tile_step = step(dve.tensor_reduce(ntile[:], above[:], AX_X, ALU.add))
                dve.wait_ge(dve_step, rank_step)
                rank_step = step(rank_to_int(B - 1))
                dve.wait_ge(dve_step, tile_step)
                tile_step = step(dve.tensor_tensor_scan(incl[:], ntile[:], zeros_e[:], 0.0, ALU.add, ALU.add))
                dve.wait_ge(dve_step, rank_step)
                rank_row(B - 1).then_inc(row_made, 1)
                dve.wait_ge(dve_step, tile_step)
                tile_step = step(dve.tensor_tensor(excl[:], incl[:], ntile[:], ALU.subtract))
                rank_step = step(rank_tile(B - 1))
                dve.wait_ge(dve_step, tile_step)
                link(dve.tensor_tensor(picked[:], onehot[:], excl[:].unsqueeze(1).unsqueeze(1)
                                       .broadcast_to([P, NT, TOP_K, E]), ALU.mult))
                link(dve.tensor_reduce(start_t[:], picked[:].rearrange("p t k e -> p (t k) e"), AX_X, ALU.add))
                link(dve.tensor_tensor(slot_t[:], start_t[:], rank_t[:], ALU.add))
                dve.tensor_tensor(in_tile[:], iota_t[:].unsqueeze(1).broadcast_to([P, J, NS]),
                                  slot_t[:].unsqueeze(2).broadcast_to([P, J, NS]), ALU.is_equal
                                  ).then_inc(in_tile_made, 1)
                dve.wait_ge(in_tile_made, f + 1)
                dve.tensor_tensor(mark[:, 1, :, :], in_tile[:],
                                  place_id[:].unsqueeze(2).broadcast_to([P, J, NS]),
                                  ALU.mult).then_inc(mark_made, 1)
                row_hots(f, B - 1)
                if f == 0:
                    tile_experts(f)
                dve.wait_ge(list_done, f + 1)
                link(dve.tensor_scalar(place_lo[:], list_ps[:, 0, :], float(NO_PAIR), None, ALU.add))
                link(dve.tensor_tensor(place[:], list_ps[:, 1, :], place_lo[:], ALU.add))
                dve.tensor_single_scalar(tok[:], place[:], T - 1, ALU.bitwise_and).then_inc(tok_made, 1)
                if f:
                    tile_experts(f)
                for n in halves_left:
                    split_lo(dve, n, lo_made_dve)
                count_sent(f)

            def experts(f):
                n0 = use_no[(f"exp{f}", 0)]

                def lo_rows(t, copied):
                    dve.wait_ge(tp_copied, copied)
                    dve.tensor_tensor(xt_lo[:, t % 2, :], tp_ps[(n0 + t) % 2][:],
                                      xt_hi[:, t % 2, :].bitcast(F32), ALU.subtract).then_inc(xt_made, 1)

                def bias(t, tile_no, done, used):
                    e = dve.value_load(eid[0:1, bass.ds(tile_no, 1)], min_val=0, max_val=E - 1)
                    dve.wait_ge(exp_done, done)
                    if used is not None:
                        dve.wait_ge(yrow_made, used)
                    dve.tensor_tensor(ypre[:, t % 2, :], y_ps[t % 2][:],
                                      be_bc[:, bass.ds(e * H, H)], ALU.add).then_inc(ypre_made, 1)

                def tile(t):
                    if t + 1 < NS:
                        lo_rows(t + 1, n0 + t + 2)
                    bias(t, t, f * NS + t + 1, f * NS + t - 1 if f or t >= 2 else None)

                dve.wait_ge(eid_made, f + 1)
                lo_rows(0, n0 + 1)
                for t in range(HEAD):
                    tile(t)
                with dve.Fori(0, LOOPS) as r:
                    for j in range(STEP):
                        t = HEAD + j
                        lo_rows(t + 1, r * STEP + (n0 + t + 2))
                        bias(t, r * STEP + t, r * STEP + (f * NS + t + 1), r * STEP + (f * NS + t - 1))
                for t in range(REST, NS):
                    tile(t)

            def add_z(f, i):
                if f == 0 and i < TB:
                    for k in range(TOP_K):
                        dve.wait_ge(z_first[i][k], 16)
                        done = dve.tensor_tensor(x[:, i, :], x[:, i, :], z_slot(0, i)[:, k, :], ALU.add)
                        if k + 1 < TOP_K:
                            link(done)
                    done.then_inc(x_ffn, 1)
                elif f == 0 or i in SUM_END:
                    dve.wait_ge(z_summed, NT - TB + SUM_END.index(i) + 1 if f else i - TB + 1)
                    dve.tensor_tensor(x[:, i, :], x[:, i, :], z_slot(f, i)[:, 0, :], ALU.add
                                      ).then_inc(x_ffn, 1)
                else:
                    dve.wait_ge(z_in[1][i], 16)
                    link(dve.tensor_tensor(x[:, i, :], x[:, i, :], z_slot(1, i)[:, 0, :], ALU.add))
                    dve.tensor_tensor(x[:, i, :], x[:, i, :], z_slot(1, i)[:, 1, :], ALU.add
                                      ).then_inc(x_ffn, 1)

            def add_z_batch(b):
                for i in range(TB * b, TB * (b + 1)):
                    add_z(0, i)
                dve.wait_ge(x_ffn, TB * (b + 1))

            def add_bv(b):
                dve.wait_ge(v_done, b + 1)
                if b >= 2:
                    dve.wait_ge(ot_done, b - 1)
                dve.tensor_tensor(v_ring[b % 2][:], v_ps[:, 0:TB * D].rearrange("p (t d) -> p t d", t=TB),
                                  bv_bc[:].unsqueeze(1).broadcast_to([P, TB, D]), ALU.add
                                  ).then_inc(v_made, 1)

            biases = [e for e in range(E) if e not in BE_ACT]
            for b in range(B):
                dve.wait_ge(x_in_sem[b], 16)
                moments("g0", b)
                if b:
                    normalise("g0", b - 1)
            normalise("g0", B - 1)
            for _ in range(2):
                copy_be(biases.pop(0))
            dve.wait_ge(const_made, CONSTS)
            todo = list(DVE_HALVES)
            split_lo(dve, todo.pop(0), lo_made_dve)
            for b in range(B):
                copy_be(biases.pop(0))
                if b:
                    split_rank(0, b - 1)
                choose(0, b)
                if b + 1 < B:
                    split_lo(dve, todo.pop(0), lo_made_dve)
                if b:
                    row_hots(0, b - 1)
            route(0, todo)
            experts(0)
            moments("att", 0)
            normalise("att", 0)
            add_z_batch(1)
            moments("att", 1)
            normalise("att", 1)
            dve.wait_ge(att_in, 16 * ATT_LOADS)
            for s in range(YB):
                dve.wait_ge(scattered[s], 16 * slot_uses(YB, s))
            add_bv(0)
            for b in range(B):
                dve.wait_ge(score_done, b + 1)
                if b:
                    dve.wait_ge(prob_made, TB * b)
                link(dve.tensor_reduce(smax[:], sp_ps[:].rearrange("p (q k) -> p q k", q=TB), AX_X, ALU.max))
                dve.tensor_scalar(nmax[:], smax[:], -SCALE, None, ALU.mult).then_inc(nmax_made, 1)
                if b:
                    dve.wait_ge(x_att, TB * b)
                    moments("g1", b - 1)
                if b + 2 < B:
                    add_z_batch(b + 2)
                if b:
                    normalise("g1", b - 1)
                if b + 2 < B:
                    moments("att", b + 2)
                if b + 1 < B:
                    add_bv(b + 1)
                if b + 2 < B:
                    normalise("att", b + 2)
                if b >= 2:
                    choose(1, b - 2)
                if b >= 3:
                    split_rank(1, b - 3)
                    row_hots(1, b - 3)
                dve.wait_ge(prob_made, TB * (b + 1))
                link(dve.reciprocal(pinv[:], psumrow[:]))
                for q in range(TB):
                    i = TB * b + q
                    dve.wait_ge(bo_added, i + 1)
                    dve.wait_ge(wo_done, i + 1)
                    dve.scalar_tensor_tensor(out=x[:, i, :], in0=y_ps[q][:], scalar=pinv[:, q:q + 1],
                                             in1=x[:, i, :], op0=ALU.mult, op1=ALU.add).then_inc(x_att, 1)
            dve.wait_ge(x_att, TB * B)
            moments("g1", B - 1)
            normalise("g1", B - 1)
            choose(1, B - 2)
            split_rank(1, B - 3)
            row_hots(1, B - 3)
            split_rank(1, B - 2)
            row_hots(1, B - 2)
            choose(1, B - 1)
            route(1, [])
            experts(1)
            for i in range(NT):
                add_z(1, i)


_INS = ['L0_attn_x', 'L0_attn_Wqkv', 'L0_attn_bqkv', 'L0_attn_Wo', 'L0_attn_bo',
        'L0_ffn_W_gate', 'L0_ffn_b_gate', 'L0_ffn_W_e', 'L0_ffn_b_e']


def kernel(**inputs):
    import numpy as _np
    import concourse.bacc as _bacc
    from concourse import mybir as _mybir
    from concourse.bass_utils import run_bass_kernel_spmd as _run

    nc = _bacc.Bacc("TRN2", target_bir_lowering=False, num_devices=1)
    arrays, args = {}, []
    for name in _INS:
        a = _np.ascontiguousarray(inputs[name])
        arrays[f"in_{name}_dram"] = a
        args.append(nc.dram_tensor(f"in_{name}_dram", a.shape, _mybir.dt.from_np(a.dtype),
                                   kind="ExternalInput").ap())
    out = nc.dram_tensor("out_0_dram", inputs['L0_attn_x'].shape, _mybir.dt.float32,
                         kind="ExternalOutput").ap()
    macaron_kernel(nc, *args, out)
    r = _run(nc, [arrays], core_ids=[0])
    return r.results[0]["out_0_dram"]
```
